# Optimizing a Trainium2 kernel written in Bass

```python
import numpy as np
import jax
import jax.numpy as jnp

def _softmax(x, axis=-1):
    return jax.nn.softmax(x, axis=axis)

def _gelu(x):
    return jax.nn.gelu(x, approximate=True)

def _silu(x):
    return jax.nn.silu(x)

def _sigmoid(x):
    return jax.nn.sigmoid(x)

def _layernorm(x, axis=-1, eps=1e-05):
    m = jnp.mean(x, axis=axis, keepdims=True)
    v = jnp.var(x, axis=axis, keepdims=True)
    return (x - m) / jnp.sqrt(v + eps)

def _scatter_add(tgt, idx, src, axis=0):
    return tgt.at[idx].add(src)

def _segment_sum(src, seg, n):
    return jax.ops.segment_sum(src, seg, n)
kernel_name = 'mk_gnn_resnorm_d2_gnn_r16_66db2a'

def setup_inputs(seed: int=0):
    np.random.seed(seed)
    _w = jnp.asarray

    def _rec_inputs():
        import jax
        import jax.numpy as jnp
        _gk = jax.random.key(seed)
        x = -0.0003713 + 1 * jax.random.normal(jax.random.fold_in(_gk, 1), (3125, 256), jnp.float32)
        src = jax.random.randint(jax.random.fold_in(_gk, 2), (100000,), 0, 3125, jnp.int32)
        dst = jnp.minimum((3125 * jax.random.uniform(jax.random.fold_in(_gk, 3), (100000,)) ** 2.0).astype(jnp.int32), 49999)
        _o = jnp.argsort(dst, stable=True)
        src = src[_o]
        dst = dst[_o]
        edge_type_4 = jax.random.randint(jax.random.fold_in(_gk, 12), (100000,), 0, 4, jnp.int32)
        return (x, src, dst, edge_type_4)
    x, src, dst, edge_type_4 = _rec_inputs()

    def _L0_gnn_setup():
        import jax, jax.numpy as jnp
        import numpy as np
        N_NODES = 3125
        key = jax.random.key(seed)
        k1, k2, k3 = jax.random.split(key, 3)
        x = jax.random.normal(k1, (N_NODES, 256), dtype=jnp.float32)
        W = jax.random.normal(k2, (256, 256), dtype=jnp.float32) * (1.0 / np.sqrt(256))
        edge_index = jax.random.randint(k3, (2, 100000), 0, N_NODES, dtype=jnp.int64)
        return {'x': x, 'W': W, 'edge_index': edge_index}
    _L0_gnn_all = _L0_gnn_setup()
    _L0_gnn_in = {k: v for k, v in _L0_gnn_all.items() if k in ('W',)}
    del _L0_gnn_all

    def _L1_gnn_setup():
        import jax, jax.numpy as jnp
        import numpy as np
        N_NODES = 3125
        N_EDGES = 50000
        DIM = 256
        DEPTH = 4
        N_REL = 4
        EPS = 1e-05

        def _rgcn_layer(X, W, root, bias, gamma, beta, src, dst, etype, inv_deg):
            h = jnp.einsum('ni,rio->rno', X, W)
            msg = h[etype, src] * inv_deg[:, None]
            agg = jax.ops.segment_sum(msg, dst, num_segments=X.shape[0])
            out = agg + X @ root + bias
            mu = jnp.mean(out, axis=-1, keepdims=True)
            var = jnp.mean(jnp.square(out - mu), axis=-1, keepdims=True)
            out = (out - mu) * jax.lax.rsqrt(var + EPS) * gamma + beta
            out = jax.nn.elu(out)
            return out + X
        key = jax.random.key(seed)
        ks = jax.random.split(key, 8)
        scale = 1.0 / np.sqrt(DIM)
        return {'node_embedding': jax.random.normal(ks[0], (N_NODES, DIM), jnp.float32), 'weights': jax.random.normal(ks[1], (DEPTH, N_REL, DIM, DIM), jnp.float32) * scale, 'roots': jax.random.normal(ks[2], (DEPTH, DIM, DIM), jnp.float32) * scale, 'biases': jax.random.normal(ks[3], (DEPTH, DIM), jnp.float32) * 0.01, 'ln_gamma': jnp.ones((DEPTH, DIM), jnp.float32), 'ln_beta': jnp.zeros((DEPTH, DIM), jnp.float32), 'edge_index': jax.random.randint(ks[4], (2, N_EDGES), 0, N_NODES, jnp.int32), 'edge_type': jax.random.randint(ks[5], (N_EDGES,), 0, N_REL, jnp.int32)}
    _L1_gnn_all = _L1_gnn_setup()
    _L1_gnn_in = {k: v for k, v in _L1_gnn_all.items() if k in ('weights', 'roots', 'biases', 'ln_gamma', 'ln_beta')}
    del _L1_gnn_all
    return {'x': x, 'src': src, 'dst': dst, 'edge_type_4': edge_type_4, 'L0_gnn_W': _L0_gnn_in['W'], 'L1_gnn_weights': _L1_gnn_in['weights'], 'L1_gnn_roots': _L1_gnn_in['roots'], 'L1_gnn_biases': _L1_gnn_in['biases'], 'L1_gnn_ln_gamma': _L1_gnn_in['ln_gamma'], 'L1_gnn_ln_beta': _L1_gnn_in['ln_beta']}

def reference(x, src, dst, edge_type_4, L0_gnn_W, L1_gnn_weights, L1_gnn_roots, L1_gnn_biases, L1_gnn_ln_gamma, L1_gnn_ln_beta):
    import jax
    import jax.numpy as jnp

    def _L0_gnn_ref(x, W, edge_index):
        import jax, jax.numpy as jnp
        import numpy as np
        N_NODES = 3125
        N = x.shape[0]
        src, dst = (edge_index[0], edge_index[1])
        h = x @ W
        deg = jax.ops.segment_sum(jnp.ones_like(dst, dtype=h.dtype), dst, num_segments=N)
        deg_inv_sqrt = jnp.where(deg > 0, jax.lax.rsqrt(jnp.maximum(deg, 1)), 0.0)
        norm = deg_inv_sqrt[src] * deg_inv_sqrt[dst]
        msgs = h[src] * norm[:, None]
        out = jax.ops.segment_sum(msgs, dst, num_segments=N)
        return out

    def _L1_gnn_ref(node_embedding, weights, roots, biases, ln_gamma, ln_beta, edge_index, edge_type):
        import jax, jax.numpy as jnp
        import numpy as np
        N_NODES = 3125
        N_EDGES = 50000
        DIM = 256
        DEPTH = 4
        N_REL = 4
        EPS = 1e-05

        def _rgcn_layer(X, W, root, bias, gamma, beta, src, dst, etype, inv_deg):
            h = jnp.einsum('ni,rio->rno', X, W)
            msg = h[etype, src] * inv_deg[:, None]
            agg = jax.ops.segment_sum(msg, dst, num_segments=X.shape[0])
            out = agg + X @ root + bias
            mu = jnp.mean(out, axis=-1, keepdims=True)
            var = jnp.mean(jnp.square(out - mu), axis=-1, keepdims=True)
            out = (out - mu) * jax.lax.rsqrt(var + EPS) * gamma + beta
            out = jax.nn.elu(out)
            return out + X
        src, dst = (edge_index[0], edge_index[1])
        cnt = jnp.zeros((node_embedding.shape[0], N_REL), node_embedding.dtype)
        cnt = cnt.at[dst, edge_type].add(1.0)
        inv_deg = 1.0 / jnp.maximum(cnt[dst, edge_type], 1.0)
        X = node_embedding
        for l in range(DEPTH):
            X = _rgcn_layer(X, weights[l], roots[l], biases[l], ln_gamma[l], ln_beta[l], src, dst, edge_type, inv_deg)
        return X
    edge_index = jnp.stack([src, dst])
    x = _layernorm(x + _L0_gnn_ref(x, L0_gnn_W, edge_index), axis=-1)
    x = _layernorm(x + _L1_gnn_ref(x, L1_gnn_weights, L1_gnn_roots, L1_gnn_biases, L1_gnn_ln_gamma, L1_gnn_ln_beta, edge_index, edge_type_4), axis=-1)
    return x

_drawn_inputs = setup_inputs


def setup_inputs(seed=0):
    import zlib

    import numpy as np

    out = dict(_drawn_inputs(seed))
    spreads = {'L1_gnn_ln_gamma': (1.0, 0.2), 'L1_gnn_ln_beta': (0.0, 0.1)}
    factors = {'L1_gnn_biases': 8.0}
    for name, (base, spread) in spreads.items():
        noise = np.random.default_rng([zlib.crc32(name.encode()), seed]).standard_normal(out[name].shape)
        drawn = base * np.exp(spread * noise) if base else spread * noise
        out[name] = jnp.asarray(drawn.astype(out[name].dtype))
    for name, factor in factors.items():
        out[name] = (out[name] * factor).astype(out[name].dtype)
    return out
```

```python
import concourse.bass as bass
from concourse import mybir
from contextlib import ExitStack


def build_program(nc, x, src, dst, etype, w0, weights, roots, biases, gammas, betas, out,
                  h0_table, h_table, inv_dram):
    f32, f16, i32 = mybir.dt.float32, mybir.dt.float16, mybir.dt.int32
    ALU = mybir.AluOpType
    ACT = mybir.ActivationFunctionType
    AXX = mybir.AxisListType.X

    N, D = x.shape
    E = src.shape[0]
    L, R = weights.shape[0], weights.shape[1]
    P = 128
    NW = -(-N // P)
    TAIL = N - (NW - 1) * P
    NPAD = NW * P
    KT = D // P
    EP = 125
    EC = E // EP
    assert EP * EC == E
    NT = (E + NW * (P - 1)) // P
    HALF = 13
    BODY = 2 * HALF
    NG = NT // BODY
    assert NG * BODY == NT
    MT = NT + HALF
    RING = HALF
    NPS = 4
    SR, SU = 4, 8
    HB = NT // 2
    assert HB * 2 == NT and HB <= 512 and EC % SU == 0
    CW = 5
    NC = NW // CW
    CD = CW * D
    EPS = 1e-5
    LOWBITS = 9
    LOW = 1 << LOWBITS

    ctx = ExitStack()
    with ctx:
        def sb(name, shape, dt=f32):
            return ctx.enter_context(nc.sbuf_tensor(name, shape, dt))

        def sem(name):
            return ctx.enter_context(nc.semaphore(name))

        ident = sb("ident", [P, P])
        ones = sb("ones", [P, P])
        before = sb("before", [EP, EP])
        iota = sb("iota", [P, R * P])
        iota16 = sb("iota16", [P, NT], f16)
        zeros16 = sb("zeros16", [P, 512], f16)
        g_src = sb("g_src", [P, NT], i32)
        g_rel = sb("g_rel", [P, NT], i32)
        node = sb("node", [P, MT])
        key = sb("key", [P, NT])
        weight = sb("weight", [P, MT])
        win_f = sb("win_f", [P, NT])
        win_i = sb("win_i", [1, NT], i32)
        dis = sb("dis", [P, NW])
        X = sb("X", [P, NW * D])
        arena = sb("arena", [P, 12800 + 6400])
        X1 = arena[:, 0:NW * D]
        expo = arena[:, 6400:6400 + CD]
        acc = arena[:, 12800:12800 + NW * D]
        inv_b = arena[:, 0:R * NPAD]
        msg = sb("msg", [P, RING, D])
        idx = sb("idx", [P, BODY], i32)
        emat = sb("emat", [P, BODY, P])
        found = sb("found", [P, 2, R, P], f16)
        w0_sb = sb("w0_sb", [P, KT, D])
        w_sb = sb("w_sb", [P, KT, R, D])
        root_sb = sb("root_sb", [P, KT, D])
        bias_sb = sb("bias_sb", [1, D])
        gamma_sb = sb("gamma_sb", [P, D])
        beta_sb = sb("beta_sb", [P, D])
        xt = sb("xt", [P, 2, D])
        hout = sb("hout", [P, CW, R * D])
        stats = sb("stats", [P, NW, 6])
        mean = sb("mean", [P, NW])
        gap = sb("gap", [P, NW])
        sd = sb("sd", [P, NW])
        rstd = sb("rstd", [P, NW])
        nmr = sb("nmr", [P, NW])
        at = [0]

        def tmp(cols, dt=f32):
            a = arena[0:EP, at[0]:at[0] + cols]
            at[0] += cols
            return a if dt is f32 else a.bitcast(dt)

        src_i, dst_i, typ_i = tmp(EC, i32), tmp(EC, i32), tmp(EC, i32)
        t1_i, t2_i = tmp(EC, i32), tmp(EC, i32)
        d_hi, d_lo, val_a, val_b, rel_win = tmp(EC), tmp(EC), tmp(EC), tmp(EC), tmp(EC)
        pos, pos_hi, pos_lo = tmp(EC), tmp(EC), tmp(EC)
        hit, run, one_row = tmp(EC), tmp(EC), tmp(EC)
        tile_hot = tmp(SR * NT // 2, f16).rearrange("p (s n) -> p s n", s=SR)
        slot_a = tmp(SR * P // 2, f16).rearrange("p (s n) -> p s n", s=SR)
        slot_b = tmp(SR * P // 2, f16).rearrange("p (s n) -> p s n", s=SR)
        slot_d = tmp(SR * P // 2, f16).rearrange("p (s n) -> p s n", s=SR)
        rw_hot = tmp(SR * R * NW // 2, f16).rearrange("p (s n) -> p s n", s=SR)
        assert at[0] <= 19200
        a_i = msg[:, 0:4, :].rearrange("p a b -> p (a b)")[:, 0:NT].bitcast(i32)
        b_i = msg[:, 4:8, :].rearrange("p a b -> p (a b)")[:, 0:NT].bitcast(i32)
        c_i = msg[:, 8:12, :].rearrange("p a b -> p (a b)")[:, 0:NT].bitcast(i32)
        tot = sb("tot", [P, NW])
        n_tiles_i = sb("n_tiles_i", [P, NW], i32)
        n_tiles = sb("n_tiles", [P, NW])
        t_end = sb("t_end", [P, NW])
        t_start = sb("t_start", [P, NW])
        run0 = sb("run0", [P, NW])
        cnt = sb("cnt", [P, R * NW])
        inv = sb("inv", [P, R * NW])
        inv_t = sb("inv_t", [R * NW, P])
        deg = sb("deg", [P, NW])
        deg1 = sb("deg1", [P, NW])
        deg_s = sb("deg_s", [P, NW])

        banks = [ctx.enter_context(nc.psum_tensor(f"bank{i}", [P, 512], f32)) for i in range(8)]
        agg_ps = banks[0:NPS]
        xt_ps = banks[0:2]
        root_ps = banks[2:4]
        rel_ps = [banks[4:6], banks[6:8]]
        sa_ps, sb_ps, cnt_ps, misc_ps, inv_ps = banks[0:2], banks[2:4], banks[4], banks[5], banks[6]

        s_edges = sem("s_edges")
        s_x = sem("s_x")
        s_w0 = sem("s_w0")
        s_w = sem("s_w")
        s_gb = sem("s_gb")
        s_const = sem("s_const")
        s_pool = sem("s_pool")
        s_dve = sem("s_dve")
        s_tot = sem("s_tot")
        s_base = sem("s_base")
        s_hot = sem("s_hot")
        s_sort_mm = sem("s_sort_mm")
        s_sorted = sem("s_sorted")
        s_inv = sem("s_inv")
        s_inv_t = sem("s_inv_t")
        s_inv_s = sem("s_inv_s")
        s_inv_w = sem("s_inv_w")
        s_inv_b = sem("s_inv_b")
        s_deg = sem("s_deg")
        s_degs = sem("s_degs")
        s_dis = sem("s_dis")
        s_xpad = sem("s_xpad")
        s_tp = sem("s_tp")
        s_xt = sem("s_xt")
        s_hmm = sem("s_hmm")
        s_hev = sem("s_hev")
        s_hw = [sem(f"s_hw{j}") for j in range(CW)]
        s_idx = sem("s_idx")
        s_msg = [sem(f"s_msg{k}") for k in range(RING)]
        s_em = sem("s_em")
        s_mm = sem("s_mm")
        s_acc = sem("s_acc")
        s_stat = sem("s_stat")
        s_sd = sem("s_sd")
        s_rstd = sem("s_rstd")
        s_norm = sem("s_norm")
        s_min = sem("s_min")
        s_exp = sem("s_exp")
        s_xr = sem("s_xr")
        s_apart = sem("s_apart")
        s_out = sem("s_out")

        MM0 = BODY
        ACC0 = NPS
        BUF = 2

        block = ctx.enter_context(nc.Block())

        def cols(tensor, start, n):
            return tensor[:, bass.ds(start, n)]

        def apart(eng):
            eng.sem_inc(s_apart, 1)

        @block.sync
        def _(sp):
            for lst, at_ in ((src, src_i), (dst, dst_i), (etype, typ_i)):
                sp.dma_start(at_, lst.rearrange("(p t) -> p t", p=EP)).then_inc(s_edges, 16)
            xv = X[:, :].rearrange("p (w d) -> p w d", w=NW)
            sp.dma_start(xv[:, 0:NW - 1, :],
                         x[0:(NW - 1) * P, :].rearrange("(w p) d -> p w d", p=P)).then_inc(s_x, 16)
            sp.wait_ge(s_xpad, 1)
            sp.dma_start(xv[0:TAIL, NW - 1, :], x[(NW - 1) * P:N, :]).then_inc(s_x, 16)
            sp.dma_start(w0_sb[:, :, :], w0.rearrange("(k p) o -> p k o", p=P)).then_inc(s_w0, 16)

            def load_weights(l):
                for k in range(KT):
                    sp.dma_start(w_sb[:, k, :, :],
                                 weights[bass.ds(l, 1), :, k * P:(k + 1) * P, :]
                                 .rearrange("l r p o -> p (l r) o")).then_inc(s_w, 16)
                sp.dma_start(root_sb[:, :, :],
                             roots[bass.ds(l, 1), :, :].rearrange("l (k p) o -> p (l k) o", p=P)
                             ).then_inc(s_w, 16)
                sp.dma_start(bias_sb[:, :], biases[bass.ds(l, 1), :]).then_inc(s_w, 16)

            def load_affine(l):
                for v, to in ((gammas, gamma_sb), (betas, beta_sb)):
                    sp.dma_start(to[:, :], v[bass.ds(l, 1), :].to_broadcast([P, D])
                                 ).then_inc(s_gb, 16)

            load_weights(0)
            load_affine(0)
            sp.wait_ge(s_inv_s, 1)
            sp.dma_start(inv_dram[:, :], inv_t[:, :]).then_inc(s_inv_w, 16)
            sp.wait_ge(s_inv_w, 16)
            sp.dma_start(inv_b, inv_dram.rearrange("(a r) d -> a (r d)", a=1)
                         .to_broadcast([P, R * NPAD])).then_inc(s_inv_b, 16)

            h0_view = h0_table.rearrange("(w p) o -> w p o", p=P)
            h_view = h_table.rearrange("(r w p) o -> w p r o", r=R, p=P)

            def store_products(hq, first):
                with sp.Fori(0, NC) as c:
                    for j in range(CW):
                        sp.wait_ge(s_hev, hq * NW + c * CW + (BUF + j + 1))
                        if first:
                            sp.dma_start(h0_view[bass.ds(c * CW + j, 1), :, :]
                                         .rearrange("w p o -> (w p) o"),
                                         hout[:, j, 0:D]).then_inc(s_hw[j], 16)
                        else:
                            sp.dma_start(h_view[bass.ds(c * CW + j, 1), :, :, :]
                                         .rearrange("w p r o -> (w p) r o"),
                                         hout[:, j, :].rearrange("p (r o) -> p r o", r=R)
                                         ).then_inc(s_hw[j], 16)

            store_products(0, True)
            store_products(1, False)
            with sp.Fori(1, L) as q:
                sp.wait_ge(s_hmm, q * NW + (BUF + NW))
                load_weights(q)
                store_products(q + 1, False)
                sp.wait_ge(s_xr, (q + 1) * NC)
                load_affine(q)
            ov = acc.rearrange("p (w d) -> p w d", w=NW)
            sp.wait_ge(s_norm, (L + 2) * NC)
            sp.dma_start(out[0:(NW - 1) * P, :].rearrange("(w p) d -> p w d", p=P),
                         ov[:, 0:NW - 1, :]).then_inc(s_out, 16)
            sp.dma_start(out[(NW - 1) * P:N, :], ov[0:TAIL, NW - 1, :]).then_inc(s_out, 16)
            sp.wait_ge(s_out, 32)

        @block.gpsimd
        def _(pool):
            pool.memset(X[:, (NW - 1) * D:NW * D], 0.0).then_inc(s_xpad, 1)
            pool.iota(iota[:, :], [[1, R * P]], base=0, channel_multiplier=0,
                      allow_small_or_imprecise_dtypes=True)
            pool.iota(iota16[:, :], [[1, NT]], base=0, channel_multiplier=0,
                      allow_small_or_imprecise_dtypes=True)
            pool.memset(zeros16[:, :], 0.0)
            pool.memset(ones[:, :], 1.0)
            pool.memset(before[:, :], 1.0).then_inc(s_pool, 1)
            pool.memset(ident[:, :], 0.0).then_inc(s_pool, 1)
            pool.wait_ge(s_pool, 1)
            pool.affine_select(out=before[:, :], in_=before[:, :], compare_op=ALU.is_gt, fill=0.0,
                               base=0, pattern=[[1, EP]], channel_multiplier=-1)
            pool.wait_ge(s_pool, 2)
            pool.affine_select(out=ident[:, :], in_=ident[:, :], compare_op=ALU.not_equal,
                               fill=1.0, base=0, pattern=[[-1, P]], channel_multiplier=1
                               ).then_inc(s_const, 1)

            def gather(q, table):
                for j in range(CW):
                    pool.wait_ge(s_hw[j], (q + 1) * (16 * NC))
                apart(pool)
                with pool.Fori(0, NG) as g:
                    for k in range(BODY):
                        if k % HALF == 0:
                            pool.wait_ge(s_idx, q * (2 * NG) + g * 2 + (k // HALF + 1))
                        pool.wait_ge(s_mm, q * NT + g * BODY + (MM0 + k + 1 - RING))
                        apart(pool)
                        pool.indirect_dma_start(
                            out=msg[:, k % RING, :], out_offset=None, in_=table[:, :],
                            in_offset=bass.IndirectOffsetOnAxis(ap=idx[:, k:k + 1], axis=0)
                        ).then_inc(s_msg[k % RING], 16)

            gather(0, h0_table)
            with pool.Fori(1, L) as q:
                gather(q, h_table)
            gather(L, h_table)

        @block.tensor
        def _(pe):
            pe.wait_ge(s_const, 1)
            pe.wait_ge(s_tot, 1)
            pe.matmul(misc_ps[0:EP, 0:NW], before[:, :], tot[0:EP, :], start=True, stop=True
                      ).then_inc(s_mm, MM0)
            pe.matmul(misc_ps[:, 64:64 + NW], ones[0:EP, :], tot[0:EP, :],
                      start=True, stop=True).then_inc(s_base, 1)
            sums = [(sa_ps[0], HB), (sa_ps[1], HB), (sb_ps[0], HB), (sb_ps[1], HB),
                    (cnt_ps, R * NW)]
            for ps, n in sums:
                mm = pe.matmul(ps[:, 0:n], zeros16[0:EP, 0:P], zeros16[0:EP, 0:n],
                               start=True, stop=False)
            mm.then_inc(s_sort_mm, SR)
            pe.sem_inc(s_hmm, BUF)
            with pe.Fori(0, EC // SU) as i:
                for k in range(SU):
                    s = k % SR
                    pe.wait_ge(s_hot, i * SU + (k + 1))
                    for b in range(2):
                        hot = tile_hot[:, s, b * HB:(b + 1) * HB]
                        pe.matmul(sa_ps[b][:, 0:HB], slot_a[:, s, :], hot, start=False, stop=False)
                    for b in range(2):
                        hot = tile_hot[:, s, b * HB:(b + 1) * HB]
                        pe.matmul(sb_ps[b][:, 0:HB], slot_b[:, s, :], hot, start=False, stop=False)
                    pe.matmul(cnt_ps[:, 0:R * NW], slot_d[:, s, :], rw_hot[:, s, :],
                              start=False, stop=False).then_inc(s_sort_mm, 1)
            for ps, n in sums:
                mm = pe.matmul(ps[:, 0:n], zeros16[0:EP, 0:P], zeros16[0:EP, 0:n],
                               start=False, stop=True)
            mm.then_inc(s_sorted, 1)
            pe.wait_ge(s_inv, 1)
            pe.transpose(inv_ps[0:R * NW, 0:P], inv[:, :], ident[:, :]).then_inc(s_inv_t, 1)

            def transpose_window(hq, c, j):
                n = hq * NW + c * CW + j
                pe.wait_ge(s_xt, n + (BUF if j == 0 else BUF - 1))
                for k in range(KT):
                    tp = pe.transpose(xt_ps[j % 2][:, k * P:(k + 1) * P],
                                      X[:, c * CD + j * D + k * P:c * CD + j * D + (k + 1) * P],
                                      ident[:, :])
                tp.then_inc(s_tp, 1)

            def multiply_window(hq, c, j, first):
                n = hq * NW + c * CW + j
                pe.wait_ge(s_xt, n + (BUF + 1))
                pe.wait_ge(s_hev, n + (BUF if j == 0 else BUF - 1))
                xk = [xt[:, j % 2, k * P:(k + 1) * P] for k in range(KT)]
                if first:
                    for k in range(KT):
                        mm = pe.matmul(rel_ps[j % 2][0][:, 0:D], xk[k], w0_sb[:, k, :],
                                       start=(k == 0), stop=(k == KT - 1))
                else:
                    for h in range(2):
                        for k in range(KT):
                            pe.matmul(rel_ps[j % 2][h][:, :], xk[k],
                                      w_sb[:, k, 2 * h:2 * h + 2, :].rearrange("p r o -> p (r o)"),
                                      start=(k == 0), stop=(k == KT - 1))
                    for k in range(KT):
                        pe.matmul(root_ps[j % 2][:, 0:D], xk[k], root_sb[:, k, :],
                                  start=(k == 0), stop=False)
                    mm = pe.matmul(root_ps[j % 2][:, 0:D], ones[0:1, :], bias_sb[:, :],
                                   start=False, stop=True)
                mm.then_inc(s_hmm, 1)

            def products(hq, first):
                if first:
                    pe.wait_ge(s_x, 32)
                    pe.wait_ge(s_w0, 16)
                    pe.wait_ge(s_dis, 1)
                else:
                    pe.wait_ge(s_w, hq * (16 * (KT + 2)))
                for c in range(NC):
                    if not first:
                        pe.wait_ge(s_xr, (hq - 1) * NC + c + 1)
                    transpose_window(hq, c, 0)
                    for j in range(CW):
                        if j + 1 < CW:
                            transpose_window(hq, c, j + 1)
                        multiply_window(hq, c, j, first)

            def aggregate(q):
                pe.wait_ge(s_hev, q * NW + (BUF + NW))
                apart(pe)
                with pe.Fori(0, NG) as g:
                    for k in range(BODY):
                        pe.wait_ge(s_em, q * MT + g * BODY + (k + 1))
                        pe.wait_ge(s_msg[k % RING],
                                   (q * (2 * NG) + g * 2 + (k // RING + 1)) * 16)
                        lag = 2 if k < 2 else NPS
                        pe.wait_ge(s_acc, q * NT + g * BODY + (ACC0 + k + 1 - lag))
                        pe.matmul(agg_ps[k % NPS][:, 0:D], emat[:, k, :], msg[:, k % RING, :],
                                  start=True, stop=True).then_inc(s_mm, 1)

            products(0, True)
            aggregate(0)
            products(1, False)
            with pe.Fori(1, L) as q:
                aggregate(q)
                products(q + 1, False)
            aggregate(L)

        @block.scalar
        def _(act):
            act.sem_inc(s_xt, BUF)
            act.sem_inc(s_hev, BUF)
            act.wait_ge(s_deg, 1)
            act.activation(deg_s[:, :], deg1[:, :], ACT.Sqrt).then_inc(s_degs, 1)

            def copy_transpose(hq, c, j):
                n = hq * NW + c * CW + j
                act.wait_ge(s_tp, n + 1)
                act.wait_ge(s_hmm, n + (BUF if j == 0 else BUF - 1))
                act.copy(xt[:, j % 2, :], xt_ps[j % 2][:, 0:D]).then_inc(s_xt, 1)

            def copy_products(hq, c, j, first, stored):
                n = hq * NW + c * CW + j
                act.wait_ge(s_hmm, n + (BUF + 1))
                if stored:
                    act.wait_ge(s_hw[j], (hq * NC + c) * 16)
                if first:
                    act.activation(hout[:, j, 0:D], rel_ps[j % 2][0][:, 0:D], ACT.Identity,
                                   scale=cols(dis, c * CW + j, 1)).then_inc(s_hev, 1)
                else:
                    for h in range(2):
                        act.copy(hout[:, j, h * 2 * D:(h + 1) * 2 * D], rel_ps[j % 2][h][:, :])
                    act.copy(cols(acc, c * CD + j * D, D), root_ps[j % 2][:, 0:D]
                             ).then_inc(s_hev, 1)

            def copy_chunk(hq, c, first=False, stored=True):
                copy_transpose(hq, c, 0)
                for j in range(CW):
                    if j + 1 < CW:
                        copy_transpose(hq, c, j + 1)
                    copy_products(hq, c, j, first, stored)

            def copy_rows(q, table):
                with act.Fori(0, NG) as g:
                    for h in range(2):
                        act.wait_ge(s_mm, q * NT + g * BODY + (MM0 - HALF + h * HALF))
                        act.copy(idx[:, h * HALF:(h + 1) * HALF],
                                 cols(table, g * BODY + h * HALF, HALF)).then_inc(s_idx, 1)

            def root_of_variance(q):
                act.wait_ge(s_stat, q + 1)
                act.activation(sd[:, :], sd[:, :], ACT.Sqrt).then_inc(s_sd, 1)
                act.wait_ge(s_rstd, q + 1)

            def normalise(c, to):
                for j in range(CW):
                    a = act.activation(cols(to, c * CD + j * D, D), cols(acc, c * CD + j * D, D),
                                       ACT.Identity, bias=cols(nmr, c * CW + j, 1),
                                       scale=cols(rstd, c * CW + j, 1))
                a.then_inc(s_norm, 1)

            def exponentials(q, c):
                act.wait_ge(s_min, (q - 1) * NC + c + 1)
                act.activation(expo, expo, ACT.Exp).then_inc(s_exp, 1)

            act.wait_ge(s_dis, 1)
            copy_chunk(0, 0, True, stored=False)
            with act.Fori(1, NC) as c:
                copy_chunk(0, c, True)
            copy_rows(0, g_src)
            root_of_variance(0)
            normalise(0, X)
            with act.Fori(1, NC) as c:
                normalise(c, X)
                copy_chunk(1, c - 1)
            copy_chunk(1, NC - 1)
            with act.Fori(1, L) as q:
                copy_rows(q, g_rel)
                root_of_variance(q)
                normalise(0, acc)
                normalise(1, acc)
                exponentials(q, 0)
                with act.Fori(2, NC) as c:
                    normalise(c, acc)
                    exponentials(q, c - 1)
                    copy_chunk(q + 1, c - 2)
                exponentials(q, NC - 1)
                copy_chunk(q + 1, NC - 2)
                copy_chunk(q + 1, NC - 1)
            copy_rows(L, g_rel)
            root_of_variance(L)
            normalise(0, acc)
            with act.Fori(1, NC) as c:
                normalise(c, acc)
                exponentials(L, c - 1)
            exponentials(L, NC - 1)
            root_of_variance(L + 1)
            with act.Fori(0, NC) as c:
                normalise(c, acc)

        @block.vector
        def _(dve):
            steps = [0]

            def done(ins, more=0):
                steps[0] += 1
                ins.then_inc(s_dve, 1)
                dve.wait_ge(s_dve, more + steps[0])

            dve.memset(one_row, 1.0)
            dve.wait_ge(s_edges, 48)
            dve.wait_ge(s_const, 1)
            done(dve.tensor_scalar(t1_i, dst_i, 7, None, ALU.arith_shift_right))
            dve.tensor_copy(d_hi, t1_i)
            done(dve.scalar_tensor_tensor(rel_win, typ_i, float(NW), t1_i, ALU.mult, ALU.add))
            done(dve.tensor_scalar(t1_i, dst_i, P - 1, None, ALU.bitwise_and))
            dve.tensor_copy(d_lo, t1_i)
            done(dve.tensor_scalar(t1_i, t1_i, 3, None, ALU.logical_shift_left))
            done(dve.tensor_scalar(t2_i, src_i, LOWBITS, None, ALU.arith_shift_right))
            done(dve.tensor_tensor(t1_i, t1_i, t2_i, ALU.bitwise_or))
            done(dve.tensor_scalar(val_b, t1_i, 1.0, None, ALU.add))
            done(dve.tensor_scalar(t2_i, src_i, LOW - 1, 2, ALU.bitwise_and,
                                   ALU.logical_shift_left))
            done(dve.tensor_tensor(t2_i, t2_i, typ_i, ALU.bitwise_or))
            dve.tensor_copy(val_a, t2_i)
            with dve.Fori(0, NW) as w:
                c = dve.tensor_scalar(hit, d_hi, iota[0:EP, bass.ds(w, 1)], None,
                                      ALU.is_equal, ALU.add, accum_out=tot[0:EP, bass.ds(w, 1)])
                c.then_inc(s_dve, 1)
                dve.wait_ge(s_dve, w + (steps[0] + 1))
            steps[0] += NW
            done(dve.memset(pos, 0.0))
            dve.sem_inc(s_tot, 1)
            dve.wait_ge(s_base, 1)
            done(dve.tensor_scalar(n_tiles_i[:, :], misc_ps[:, 64:64 + NW], float(P - 1), None,
                                   ALU.add))
            done(dve.tensor_scalar(n_tiles_i[:, :], n_tiles_i[:, :], 7, None,
                                   ALU.arith_shift_right))
            done(dve.tensor_copy(n_tiles[:, :], n_tiles_i[:, :]))
            done(dve.tensor_tensor_scan(t_end[:, :], ones[:, 0:NW], n_tiles[:, :], 0.0,
                                        ALU.mult, ALU.add))
            done(dve.tensor_tensor(t_start[:, :], t_end[:, :], n_tiles[:, :], ALU.subtract))
            done(dve.scalar_tensor_tensor(run0[0:EP, :], t_start[0:EP, :], float(P),
                                          misc_ps[0:EP, 0:NW], ALU.mult, ALU.add))
            done(dve.tensor_scalar(run0[0:EP, :], run0[0:EP, :], -1.0, None, ALU.add))
            n0 = steps[0]
            with dve.Fori(0, NW) as w:
                steps[0] = n0
                m = w * 4
                done(dve.tensor_scalar(hit, d_hi, iota[0:EP, bass.ds(w, 1)], None,
                                       ALU.is_equal), m)
                done(dve.tensor_tensor_scan(run, one_row, hit, run0[0:EP, bass.ds(w, 1)],
                                            ALU.mult, ALU.add), m)
                done(dve.tensor_tensor(run, run, hit, ALU.mult), m)
                done(dve.tensor_tensor(pos, pos, run, ALU.add), m)
            steps[0] = n0 + 4 * NW
            done(dve.tensor_copy(t1_i, pos))
            done(dve.tensor_scalar(t2_i, t1_i, 7, None, ALU.arith_shift_right))
            done(dve.tensor_copy(pos_hi, t2_i))
            done(dve.tensor_scalar(t2_i, t1_i, P - 1, None, ALU.bitwise_and))
            done(dve.tensor_copy(pos_lo, t2_i))
            lane = iota[0:EP, 0:P]
            with dve.Fori(0, EC // SU) as i:
                for k in range(SU):
                    s = k % SR
                    t = i * SU + k

                    def at_t(v):
                        return v[:, bass.ds(t, 1)]

                    dve.wait_ge(s_sort_mm, i * SU + (k + 1))
                    dve.tensor_scalar(tile_hot[:, s, :], iota16[0:EP, :], at_t(pos_hi), None,
                                      ALU.is_equal)
                    dve.tensor_scalar(slot_a[:, s, :], lane, at_t(pos_lo), at_t(val_a),
                                      ALU.is_equal, ALU.mult)
                    dve.tensor_scalar(slot_b[:, s, :], lane, at_t(pos_lo), at_t(val_b),
                                      ALU.is_equal, ALU.mult)
                    dve.tensor_scalar(slot_d[:, s, :], lane, at_t(d_lo), None, ALU.is_equal)
                    dve.tensor_scalar(rw_hot[:, s, :], iota16[0:EP, 0:R * NW], at_t(rel_win),
                                      None, ALU.is_equal).then_inc(s_hot, 1)
            dve.wait_ge(s_sorted, 1)
            done(dve.tensor_copy(cnt[:, :], cnt_ps[:, 0:R * NW]))
            done(dve.tensor_scalar(inv[:, :], cnt[:, :], 1.0, None, ALU.max))
            dve.reciprocal(inv[:, :], inv[:, :]).then_inc(s_inv, 1)
            done(dve.tensor_reduce(deg[:, :], cnt[:, :].rearrange("p (r w) -> p w r", r=R),
                                   AXX, ALU.add))
            dve.tensor_scalar(deg1[:, :], deg[:, :], 1.0, None, ALU.max).then_inc(s_deg, 1)
            for b in range(2):
                half = slice(b * HB, (b + 1) * HB)
                dve.tensor_copy(a_i[:, half], sa_ps[b][:, 0:HB])
                dve.tensor_scalar(b_i[:, half], sb_ps[b][:, 0:HB], -1.0, None, ALU.add)
                done(dve.tensor_scalar(c_i[:, half], sb_ps[b][:, 0:HB], -1.0, 0.0, ALU.add,
                                       ALU.max))
            done(dve.tensor_scalar(b_i, b_i, 3, None, ALU.arith_shift_right))
            done(dve.memset(node[:, NT:MT], -1.0))
            done(dve.memset(weight[:, NT:MT], 0.0))
            done(dve.tensor_copy(node[:, 0:NT], b_i))
            done(dve.tensor_scalar(c_i, c_i, 7, LOWBITS, ALU.bitwise_and,
                                   ALU.logical_shift_left))
            done(dve.tensor_scalar(b_i, a_i, 2, None, ALU.arith_shift_right))
            done(dve.tensor_tensor(g_src[:, :], b_i, c_i, ALU.bitwise_or))
            done(dve.tensor_scalar(a_i, a_i, 3, None, ALU.bitwise_and))
            dve.scalar_tensor_tensor(g_rel[:, :], a_i, float(NPAD), g_src[:, :],
                                     ALU.mult, ALU.add)
            done(dve.scalar_tensor_tensor(key[:, :], a_i, float(P), node[:, 0:NT],
                                          ALU.mult, ALU.add))
            dve.wait_ge(s_inv_t, 1)
            dve.tensor_copy(inv_t[:, :], inv_ps[0:R * NW, 0:P]).then_inc(s_inv_s, 1)
            dve.wait_ge(s_degs, 1)
            done(dve.reciprocal(deg_s[:, :], deg_s[:, :]))
            dve.scalar_tensor_tensor(dis[:, :], deg[:, :], 0.0, deg_s[:, :],
                                     ALU.is_gt, ALU.mult).then_inc(s_dis, 1)
            done(dve.memset(win_f[:, :], -1.0))
            with dve.Fori(0, NW) as w:
                dve.scalar_tensor_tensor(win_f[:, :], iota16[:, :], t_start[:, bass.ds(w, 1)],
                                         win_f[:, :], ALU.is_ge, ALU.add).then_inc(s_dve, 1)
                dve.wait_ge(s_dve, w + (steps[0] + 1))
            steps[0] += NW
            done(dve.tensor_copy(win_i[:, :], win_f[0:1, :]))
            dve.memset(acc, 0.0).then_inc(s_acc, ACC0)

            def edge_matrix(q, t, k, first, free):
                if free is not None:
                    dve.wait_ge(s_mm, free)
                dve.tensor_scalar(emat[:, k % BODY, :], iota[:, 0:P],
                                  node[:, bass.ds(t, 1)],
                                  None if first else weight[:, bass.ds(t, 1)],
                                  ALU.is_equal, ALU.bypass if first else ALU.mult
                                  ).then_inc(s_em, 1)

            inv_v = inv_b.rearrange("p (r w d) -> p r w d", r=R, w=NW)
            key_v = iota[:, :].rearrange("p (r d) -> p r d", r=R)

            def messages(q, first):
                for k in range(HALF):
                    edge_matrix(q, k, k, first, None)
                if first:
                    dve.wait_ge(s_inv_b, 16)
                with dve.Fori(0, NG) as g:
                    for h in range(2):
                        _, wins = nc.values_load_multi_w_load_instructions(
                            win_i[0:1, bass.ds(g * BODY + h * HALF, HALF)],
                            engines=[mybir.EngineType.DVE],
                            min_val=0, max_val=NW - 1, 
                            skip_runtime_bounds_check_because="a tile's window is counted over NW windows")
                        for i in range(HALF):
                            k = h * HALF + i
                            t = g * BODY + k
                            edge_matrix(q, t + HALF, k + HALF, first,
                                        q * NT + g * BODY + (MM0 + k + HALF + 1 - BODY))
                            if first:
                                dve.scalar_tensor_tensor(
                                    found[:, k % 2, :, :], key_v, key[:, bass.ds(t, 1)],
                                    inv_v[:, :, bass.ds(wins[i], 1), :]
                                    .rearrange("p r w d -> p r (w d)"),
                                    ALU.is_equal, ALU.mult, accum_out=weight[:, bass.ds(t, 1)])
                            dve.wait_ge(s_mm, q * NT + g * BODY + (MM0 + k + 1))
                            dve.wait_ge(s_acc, q * NT + g * BODY + (ACC0 + k))
                            a = cols(acc, wins[i] * D, D)
                            dve.tensor_tensor(a, a, agg_ps[k % NPS][:, 0:D], ALU.add
                                              ).then_inc(s_acc, 1)

            def statistics(w, more):
                done(dve.bn_stats(stats[:, bass.ds(w, 1), :].rearrange("p w s -> p (w s)"),
                                  cols(acc, w * D, D)), more)

            def scales(q, more):
                mean_e, dev_e, mean_o, dev_o = (stats[:, :, k] for k in (1, 2, 4, 5))
                done(dve.tensor_tensor(mean[:, :], mean_e, mean_o, ALU.add), more)
                done(dve.tensor_scalar(mean[:, :], mean[:, :], 0.5, None, ALU.mult), more)
                done(dve.tensor_tensor(gap[:, :], mean_e, mean_o, ALU.subtract), more)
                done(dve.scalar_tensor_tensor(gap[:, :], gap[:, :], 0.25, gap[:, :],
                                              ALU.mult, ALU.mult), more)
                done(dve.tensor_tensor(sd[:, :], dev_e, dev_o, ALU.add), more)
                done(dve.scalar_tensor_tensor(sd[:, :], sd[:, :], 1.0 / D, gap[:, :],
                                              ALU.mult, ALU.add), more)
                dve.tensor_scalar(sd[:, :], sd[:, :], EPS, None, ALU.add).then_inc(s_stat, 1)
                dve.wait_ge(s_sd, q + 1)
                done(dve.reciprocal(rstd[:, :], sd[:, :]), more)
                dve.scalar_tensor_tensor(nmr[:, :], mean[:, :], -1.0, rstd[:, :],
                                         ALU.mult, ALU.mult).then_inc(s_rstd, 1)

            messages(0, True)
            dve.wait_ge(s_acc, ACC0 + NT)
            n0 = steps[0]
            with dve.Fori(0, NW) as w:
                steps[0] = n0
                done(dve.scalar_tensor_tensor(cols(acc, w * D, D), cols(acc, w * D, D),
                                              cols(dis, w, 1), cols(X, w * D, D),
                                              ALU.mult, ALU.add), w * 2)
                statistics(w, w * 2)
            steps[0] = n0 + 2 * NW
            scales(0, 0)
            with dve.Fori(0, NC) as c:
                dve.wait_ge(s_norm, c + 1)
                dve.tensor_copy(cols(X1, c * CD, CD), cols(X, c * CD, CD)).then_inc(s_xr, 1)

            def relational(q, more):
                messages(q, False)
                dve.wait_ge(s_acc, q * NT + (ACC0 + NT))
                apart(dve)
                n = steps[0]
                with dve.Fori(0, NW) as w:
                    steps[0] = n
                    statistics(w, w + more)
                steps[0] = n + NW
                scales(q, more)
                dve.wait_ge(s_gb, q * 32)
                apart(dve)
                n = steps[0]
                with dve.Fori(0, NC) as c:
                    steps[0] = n
                    m = c * 3 + more
                    y = cols(acc, c * CD, CD)
                    y3 = y.rearrange("p (w d) -> p w d", w=CW)
                    xc = cols(X, c * CD, CD)
                    dve.wait_ge(s_norm, q * NC + c + 1)
                    for v, op in ((gamma_sb, ALU.mult), (beta_sb, ALU.add)):
                        done(dve.tensor_tensor(y3, y3, v[:, :].rearrange("p (w d) -> p w d", w=1)
                                               .to_broadcast([P, CW, D]), op), m)
                    dve.tensor_scalar(expo, y, 0.0, None, ALU.min).then_inc(s_min, 1)
                    dve.wait_ge(s_exp, (q - 1) * NC + c + 1)
                    done(dve.scalar_tensor_tensor(y, y, 0.0, expo, ALU.max, ALU.add), m)
                    dve.scalar_tensor_tensor(xc, y, -1.0, xc, ALU.add, ALU.add
                                             ).then_inc(s_xr, 1)
                steps[0] = n + 3 * NC

            n0 = steps[0]
            per_layer = NW + 7 + 3 * NC
            with dve.Fori(1, L) as q:
                steps[0] = n0
                relational(q, (q - 1) * per_layer)
                assert steps[0] == n0 + per_layer
            steps[0] = n0 + (L - 1) * per_layer
            relational(L, 0)
            dve.wait_ge(s_xr, (L + 1) * NC)
            n0 = steps[0]
            with dve.Fori(0, NW) as w:
                steps[0] = n0
                done(dve.tensor_tensor(cols(acc, w * D, D), cols(X, w * D, D), cols(X1, w * D, D),
                                       ALU.add), w * 2)
                statistics(w, w * 2)
            steps[0] = n0 + 2 * NW
            scales(L + 1, 0)


_INS = ['x', 'src', 'dst', 'edge_type_4', 'L0_gnn_W', 'L1_gnn_weights', 'L1_gnn_roots',
        'L1_gnn_biases', 'L1_gnn_ln_gamma', 'L1_gnn_ln_beta']


def kernel(**inputs):
    import numpy as _np
    import concourse.bacc as _bacc
    from concourse.bass_utils import run_bass_kernel_spmd as _run

    f32 = mybir.dt.float32
    nc = _bacc.Bacc("TRN2", target_bir_lowering=False, num_devices=1)
    arrays, args = {}, []
    for name in _INS:
        a = _np.ascontiguousarray(inputs[name])
        arrays[f"in_{name}_dram"] = a
        args.append(nc.dram_tensor(f"in_{name}_dram", a.shape, mybir.dt.from_np(a.dtype),
                                   kind="ExternalInput").ap())
    n, d = inputs['x'].shape
    r = inputs['L1_gnn_weights'].shape[1]
    rows = -(-n // 128) * 128
    out = nc.dram_tensor("out_0_dram", (n, d), f32, kind="ExternalOutput").ap()
    h0_table = nc.dram_tensor("h0_table", (rows, d), f32, kind="Internal").ap()
    h_table = nc.dram_tensor("h_table", (r * rows, d), f32, kind="Internal").ap()
    inv_dram = nc.dram_tensor("inv_dram", (r * rows // 128, 128), f32, kind="Internal").ap()
    build_program(nc, *args, out, h0_table, h_table, inv_dram)
    res = _run(nc, [arrays], core_ids=[0])
    return res.results[0]["out_0_dram"]
```

```python
import concourse.bass as bass
from concourse import mybir
from contextlib import ExitStack


def build_program(nc, x, src, dst, etype, w0, weights, roots, biases, gammas, betas, out,
                  h0_table, h_table, inv_dram):
    f32, f16, i32 = mybir.dt.float32, mybir.dt.float16, mybir.dt.int32
    ALU = mybir.AluOpType
    ACT = mybir.ActivationFunctionType
    AXX = mybir.AxisListType.X

    N, D = x.shape
    E = src.shape[0]
    L, R = weights.shape[0], weights.shape[1]
    P = 128
    NW = -(-N // P)
    TAIL = N - (NW - 1) * P
    NPAD = NW * P
    KT = D // P
    EP = 125
    EC = E // EP
    assert EP * EC == E
    NT = (E + NW * (P - 1)) // P
    HALF = 13
    BODY = 2 * HALF
    NG = NT // BODY
    assert NG * BODY == NT
    MT = NT + HALF
    RING = HALF
    NPS = 4
    SB = 8
    SU = 2 * SB
    SR = 4
    HB = NT // 2
    assert HB * 2 == NT and HB <= 512 and EC % SU == 0
    CW = 5
    NC = NW // CW
    CD = CW * D
    EPS = 1e-5
    LOWBITS = 9
    LOW = 1 << LOWBITS

    ctx = ExitStack()
    with ctx:
        def sb(name, shape, dt=f32):
            return ctx.enter_context(nc.sbuf_tensor(name, shape, dt))

        def sem(name):
            return ctx.enter_context(nc.semaphore(name))

        ident = sb("ident", [P, P])
        ones = sb("ones", [P, P])
        before = sb("before", [EP, EP])
        iota = sb("iota", [P, R * P])
        iota16 = sb("iota16", [P, NT], f16)
        zeros16 = sb("zeros16", [P, 512], f16)
        g_src = sb("g_src", [P, NT], i32)
        g_rel = sb("g_rel", [P, NT], i32)
        node = sb("node", [P, MT])
        key = sb("key", [P, NT])
        weight = sb("weight", [P, MT])
        win_f = sb("win_f", [P, NT])
        win_i = sb("win_i", [1, NT], i32)
        dis = sb("dis", [P, NW])
        X = sb("X", [P, NW * D])
        arena = sb("arena", [P, 12800 + 6400])
        X1 = arena[:, 0:NW * D]
        expo = arena[:, 6400:6400 + CD]
        acc = arena[:, 12800:12800 + NW * D]
        inv_b = arena[:, 0:R * NPAD]
        msg = sb("msg", [P, RING, D])
        idx = sb("idx", [P, BODY], i32)
        emat = sb("emat", [P, BODY, P])
        found = sb("found", [P, 2, R, P], f16)
        w0_sb = sb("w0_sb", [P, KT, D])
        w_sb = sb("w_sb", [P, KT, R, D])
        root_sb = sb("root_sb", [P, KT, D])
        bias_sb = sb("bias_sb", [1, D])
        gamma_sb = sb("gamma_sb", [P, D])
        beta_sb = sb("beta_sb", [P, D])
        xt = sb("xt", [P, 2, D])
        hout = sb("hout", [P, CW, R * D])
        stats = sb("stats", [P, NW, 6])
        mean = sb("mean", [P, NW])
        gap = sb("gap", [P, NW])
        sd = sb("sd", [P, NW])
        rstd = sb("rstd", [P, NW])
        nmr = sb("nmr", [P, NW])
        x_win = sb("x_win", [P, D])
        neg_node = sb("neg_node", [P, MT])
        square = hout[:, :, :].rearrange("p a b -> p (a b)")[:, 0:HALF * P]
        at = [0]

        def tmp(cols, dt=f32):
            a = arena[0:EP, at[0]:at[0] + cols]
            at[0] += cols
            return a if dt is f32 else a.bitcast(dt)

        src_i, dst_i, typ_i = tmp(EC, i32), tmp(EC, i32), tmp(EC, i32)
        hit = src_i.bitcast(f16)[:, 0:EC]
        run, one_row = (v.bitcast(f32) for v in (dst_i, typ_i))
        t1_i, t2_i = tmp(EC, i32), tmp(EC, i32)
        d_hi, d_lo, val_a, val_b, rel_win = tmp(EC // 2, f16), tmp(EC), tmp(EC), tmp(EC), tmp(EC)
        pos, pos_hi, pos_lo = tmp(EC), tmp(EC), tmp(EC)
        tile_hot = tmp(SR * NT // 2, f16).rearrange("p (s n) -> p s n", s=SR)
        rw_hot = tmp(SU * R * NW // 2, f16).rearrange("p (b s n) -> p b s n", b=2, s=SB)
        assert at[0] <= 12800
        cells = emat[0:EP, :, :].rearrange("p a b -> p (a b)").bitcast(f16)
        batch = SB * P
        lane_hot, node_hot = (cells[:, k * 2 * batch:(k + 1) * 2 * batch]
                              .rearrange("p (b s n) -> p b s n", b=2, s=SB) for k in range(2))
        slot_a, slot_b = (cells[:, (4 + k) * batch:(5 + k) * batch]
                          .rearrange("p (s n) -> p s n", s=SB) for k in range(2))
        a_i = msg[:, 0:4, :].rearrange("p a b -> p (a b)")[:, 0:NT].bitcast(i32)
        b_i = msg[:, 4:8, :].rearrange("p a b -> p (a b)")[:, 0:NT].bitcast(i32)
        c_i = msg[:, 8:12, :].rearrange("p a b -> p (a b)")[:, 0:NT].bitcast(i32)
        tot = sb("tot", [P, NW])
        n_tiles_i = sb("n_tiles_i", [P, NW], i32)
        n_tiles = sb("n_tiles", [P, NW])
        t_end = sb("t_end", [P, NW])
        t_start = sb("t_start", [P, NW])
        run0 = sb("run0", [P, NW])
        cnt = sb("cnt", [P, R * NW])
        inv = sb("inv", [P, R * NW])
        inv_t = sb("inv_t", [R * NW, P])
        deg = sb("deg", [P, NW])
        deg1 = sb("deg1", [P, NW])
        deg_s = sb("deg_s", [P, NW])

        banks = [ctx.enter_context(nc.psum_tensor(f"bank{i}", [P, 512], f32)) for i in range(8)]
        agg_ps = banks[0:NPS]
        xt_ps = banks[0:2]
        root_t_ps, root_ps = banks[6], banks[7]
        rel_ps = [banks[4:6], banks[6:8]]
        sa_ps, sb_ps, cnt_ps, misc_ps, inv_ps = banks[0:2], banks[2:4], banks[4], banks[5], banks[6]

        s_edges = sem("s_edges")
        s_x = sem("s_x")
        s_w0 = sem("s_w0")
        s_w = sem("s_w")
        s_root = sem("s_root")
        s_gb = sem("s_gb")
        s_const = sem("s_const")
        s_pool = sem("s_pool")
        s_dve = sem("s_dve")
        s_tot = sem("s_tot")
        s_base = sem("s_base")
        s_hot = sem("s_hot")
        s_sort_mm = sem("s_sort_mm")
        s_sorted = sem("s_sorted")
        s_inv = sem("s_inv")
        s_inv_t = sem("s_inv_t")
        s_inv_s = sem("s_inv_s")
        s_inv_w = sem("s_inv_w")
        s_inv_b = sem("s_inv_b")
        s_deg = sem("s_deg")
        s_degs = sem("s_degs")
        s_dis = sem("s_dis")
        s_xpad = sem("s_xpad")
        s_tp = sem("s_tp")
        s_xt = sem("s_xt")
        s_hmm = sem("s_hmm")
        s_hev = sem("s_hev")
        s_hw = [sem(f"s_hw{j}") for j in range(CW)]
        s_idx = sem("s_idx")
        s_msg = [sem(f"s_msg{k}") for k in range(RING)]
        s_em = sem("s_em")
        s_mm = sem("s_mm")
        s_acc = sem("s_acc")
        s_stat = sem("s_stat")
        s_sd = sem("s_sd")
        s_rstd = sem("s_rstd")
        s_norm = sem("s_norm")
        s_min = sem("s_min")
        s_exp = sem("s_exp")
        s_xr = sem("s_xr")
        s_apart = sem("s_apart")
        s_h0 = sem("s_h0")
        s_lane = sem("s_lane")
        s_ab = sem("s_ab")
        s_sq = sem("s_sq")
        s_xw = sem("s_xw")
        s_rt = sem("s_rt")
        s_rx = sem("s_rx")
        s_rm = sem("s_rm")
        s_ra = sem("s_ra")
        s_zero = sem("s_zero")
        s_final = sem("s_final")
        s_out = sem("s_out")

        MM0 = BODY
        ACC0 = NPS
        BUF = 2
        SORT0 = SU

        block = ctx.enter_context(nc.Block())

        def cols(tensor, start, n):
            return tensor[:, bass.ds(start, n)]

        def apart(eng):
            eng.sem_inc(s_apart, 1)

        @block.sync
        def _(sp):
            for lst, at_ in ((src, src_i), (dst, dst_i), (etype, typ_i)):
                sp.dma_start(at_, lst.rearrange("(p t) -> p t", p=EP)).then_inc(s_edges, 16)
            xv = X[:, :].rearrange("p (w d) -> p w d", w=NW)
            sp.dma_start(xv[:, 0:NW - 1, :],
                         x[0:(NW - 1) * P, :].rearrange("(w p) d -> p w d", p=P)).then_inc(s_x, 16)
            sp.wait_ge(s_xpad, 1)
            sp.dma_start(xv[0:TAIL, NW - 1, :], x[(NW - 1) * P:N, :]).then_inc(s_x, 16)
            sp.dma_start(w0_sb[:, :, :], w0.rearrange("(k p) o -> p k o", p=P)).then_inc(s_w0, 16)

            def load_weights(l):
                for k in range(KT):
                    sp.dma_start(w_sb[:, k, :, :],
                                 weights[bass.ds(l, 1), :, k * P:(k + 1) * P, :]
                                 .rearrange("l r p o -> p (l r) o")).then_inc(s_w, 16)

            def load_root(l):
                sp.dma_start(root_sb[:, :, :],
                             roots[bass.ds(l, 1), :, :].rearrange("l (k p) o -> p (l k) o", p=P)
                             ).then_inc(s_root, 16)
                sp.dma_start(bias_sb[:, :], biases[bass.ds(l, 1), :]).then_inc(s_root, 16)

            def load_affine(l):
                for v, to in ((gammas, gamma_sb), (betas, beta_sb)):
                    sp.dma_start(to[:, :], v[bass.ds(l, 1), :].to_broadcast([P, D])
                                 ).then_inc(s_gb, 16)

            load_weights(0)
            load_root(0)
            load_affine(0)
            sp.wait_ge(s_inv_s, 1)
            sp.dma_start(inv_dram[:, :], inv_t[:, :]).then_inc(s_inv_w, 16)
            sp.wait_ge(s_inv_w, 16)
            sp.dma_start(inv_b, inv_dram.rearrange("(a r) d -> a (r d)", a=1)
                         .to_broadcast([P, R * NPAD])).then_inc(s_inv_b, 16)

            h0_view = h0_table.rearrange("(w p) o -> w p o", p=P)
            h_view = h_table.rearrange("(r w p) o -> w p r o", r=R, p=P)

            def store_products(hq, first):
                with sp.Fori(0, NC) as c:
                    for j in range(CW):
                        if first:
                            sp.wait_ge(s_h0, c * CW + (j + 1))
                        else:
                            sp.wait_ge(s_hev, hq * NW + c * CW + (BUF + j + 1))
                        if first:
                            sp.dma_start(h0_view[bass.ds(c * CW + j, 1), :, :]
                                         .rearrange("w p o -> (w p) o"),
                                         hout[:, j, 0:D]).then_inc(s_hw[j], 16)
                        else:
                            sp.dma_start(h_view[bass.ds(c * CW + j, 1), :, :, :]
                                         .rearrange("w p r o -> (w p) r o"),
                                         hout[:, j, :].rearrange("p (r o) -> p r o", r=R)
                                         ).then_inc(s_hw[j], 16)

            store_products(0, True)
            store_products(1, False)
            with sp.Fori(1, L) as q:
                sp.wait_ge(s_hmm, q * NW + (BUF + NW))
                load_weights(q)
                sp.wait_ge(s_rm, q * NW)
                load_root(q)
                store_products(q + 1, False)
                sp.wait_ge(s_xr, (q + 1) * NC)
                load_affine(q)
            ov = acc.rearrange("p (w d) -> p w d", w=NW)
            for c in range(NC):
                sp.wait_ge(s_norm, (L + 1) * NC + c + 1)
                w0_, w1 = c * CW, min((c + 1) * CW, NW - 1)
                sp.dma_start(out[w0_ * P:w1 * P, :].rearrange("(w p) d -> p w d", p=P),
                             ov[:, w0_:w1, :]).then_inc(s_out, 16)
            sp.dma_start(out[(NW - 1) * P:N, :], ov[0:TAIL, NW - 1, :]).then_inc(s_out, 16)
            sp.wait_ge(s_out, (NC + 1) * 16)

        @block.gpsimd
        def _(pool):
            pool.memset(X[:, (NW - 1) * D:NW * D], 0.0).then_inc(s_xpad, 1)
            pool.iota(iota[:, :], [[1, R * P]], base=0, channel_multiplier=0,
                      allow_small_or_imprecise_dtypes=True)
            pool.iota(iota16[:, :], [[1, NT]], base=0, channel_multiplier=0,
                      allow_small_or_imprecise_dtypes=True)
            pool.memset(zeros16[:, :], 0.0)
            pool.memset(ones[:, :], 1.0)
            pool.memset(before[:, :], 1.0).then_inc(s_pool, 1)
            pool.memset(ident[:, :], 0.0).then_inc(s_pool, 1)
            pool.wait_ge(s_pool, 1)
            pool.affine_select(out=before[:, :], in_=before[:, :], compare_op=ALU.is_gt, fill=0.0,
                               base=0, pattern=[[1, EP]], channel_multiplier=-1)
            pool.wait_ge(s_pool, 2)
            pool.affine_select(out=ident[:, :], in_=ident[:, :], compare_op=ALU.not_equal,
                               fill=1.0, base=0, pattern=[[-1, P]], channel_multiplier=1
                               ).then_inc(s_const, 1)

            def zero_sums(q):
                for c in range(NC):
                    pool.wait_ge(s_xr, (q - 1) * NC + (c + 1))
                    apart(pool)
                    pool.memset(acc[:, c * CD:(c + 1) * CD], 0.0).then_inc(s_zero, 1)

            def gather(q, table):
                for j in range(CW):
                    pool.wait_ge(s_hw[j], (q + 1) * (16 * NC))
                apart(pool)
                with pool.Fori(0, NG) as g:
                    for k in range(BODY):
                        if k % HALF == 0:
                            pool.wait_ge(s_idx, q * (2 * NG) + g * 2 + (k // HALF + 1))
                        pool.wait_ge(s_mm, q * NT + g * BODY + (MM0 + k + 1 - RING))
                        apart(pool)
                        pool.indirect_dma_start(
                            out=msg[:, k % RING, :], out_offset=None, in_=table[:, :],
                            in_offset=bass.IndirectOffsetOnAxis(ap=idx[:, k:k + 1], axis=0)
                        ).then_inc(s_msg[k % RING], 16)

            gather(0, h0_table)
            with pool.Fori(1, L) as q:
                zero_sums(q)
                gather(q, h_table)
            zero_sums(L)
            gather(L, h_table)

        @block.tensor
        def _(pe):
            pe.wait_ge(s_const, 1)
            pe.sem_inc(s_hmm, BUF)

            def transpose_window(hq, c, j):
                n = hq * NW + c * CW + j
                pe.wait_ge(s_xt, n + (BUF if j == 0 else BUF - 1))
                for k in range(KT):
                    tp = pe.transpose(xt_ps[j % 2][:, k * P:(k + 1) * P],
                                      X[:, c * CD + j * D + k * P:c * CD + j * D + (k + 1) * P],
                                      ident[:, :])
                tp.then_inc(s_tp, 1)

            def multiply_window(hq, c, j, first):
                n = hq * NW + c * CW + j
                pe.wait_ge(s_xt, n + (BUF + 1))
                pe.wait_ge(s_hev, n + (BUF if j == 0 else BUF - 1))
                xk = [xt[:, j % 2, k * P:(k + 1) * P] for k in range(KT)]
                if first:
                    for k in range(KT):
                        mm = pe.matmul(rel_ps[j % 2][0][:, 0:D], xk[k], w0_sb[:, k, :],
                                       start=(k == 0), stop=(k == KT - 1))
                else:
                    for h in range(2):
                        for k in range(KT):
                            mm = pe.matmul(rel_ps[j % 2][h][:, :], xk[k],
                                      w_sb[:, k, 2 * h:2 * h + 2, :].rearrange("p r o -> p (r o)"),
                                      start=(k == 0), stop=(k == KT - 1))
                mm.then_inc(s_hmm, 1)

            def products(hq, first):
                if first:
                    pe.wait_ge(s_x, 32)
                    pe.wait_ge(s_w0, 16)
                else:
                    pe.wait_ge(s_w, hq * (16 * KT))
                for c in range(NC):
                    if not first:
                        pe.wait_ge(s_xr, (hq - 1) * NC + c + 1)
                    transpose_window(hq, c, 0)
                    for j in range(CW):
                        if j + 1 < CW:
                            transpose_window(hq, c, j + 1)
                        multiply_window(hq, c, j, first)

            def tile_products(q, g, root):
                for k in range(BODY):
                    if root and k == 3:
                        pe.wait_ge(s_xw, (q - 1) * NW + g + 1)
                        for h in range(KT):
                            tp = pe.transpose(root_t_ps[:, h * P:(h + 1) * P],
                                              x_win[:, h * P:(h + 1) * P], ident[:, :])
                        tp.then_inc(s_rt, 1)
                    if root and k == 9:
                        pe.wait_ge(s_rx, (q - 1) * NW + g + 1)
                        pe.wait_ge(s_ra, (q - 1) * NW + g + 1)
                        for h in range(KT):
                            pe.matmul(root_ps[:, 0:D], xt[:, 0, h * P:(h + 1) * P],
                                      root_sb[:, h, :], start=(h == 0), stop=False)
                        pe.matmul(root_ps[:, 0:D], ones[0:1, :], bias_sb[:, :],
                                  start=False, stop=True).then_inc(s_rm, 1)
                    pe.wait_ge(s_em, q * MT + g * BODY + (k + 1))
                    pe.wait_ge(s_msg[k % RING],
                               (q * (2 * NG) + g * 2 + (k // RING + 1)) * 16)
                    lag = 2 if k < 2 else NPS
                    pe.wait_ge(s_acc, q * NT + g * BODY + (ACC0 + k + 1 - lag))
                    pe.matmul(agg_ps[k % NPS][:, 0:D], emat[:, k, :], msg[:, k % RING, :],
                              start=True, stop=True).then_inc(s_mm, 1)

            def aggregate(q, root=True):
                pe.wait_ge(s_hev, q * NW + (BUF + NW))
                if root:
                    pe.wait_ge(s_root, q * 32)
                apart(pe)
                if root:
                    with pe.Fori(0, NW) as g:
                        tile_products(q, g, True)
                with pe.Fori(NW if root else 0, NG) as g:
                    tile_products(q, g, False)

            products(0, True)
            pe.wait_ge(s_tot, 1)
            pe.matmul(misc_ps[0:EP, 0:NW], before[:, :], tot[0:EP, :], start=True, stop=True
                      ).then_inc(s_mm, MM0)
            pe.matmul(misc_ps[:, 64:64 + NW], ones[0:EP, :], tot[0:EP, :],
                      start=True, stop=True).then_inc(s_base, 1)
            pe.wait_ge(s_hev, BUF + NW)
            sums = [(sa_ps[0], HB), (sa_ps[1], HB), (sb_ps[0], HB), (sb_ps[1], HB),
                    (cnt_ps, R * NW)]
            for ps, n in sums:
                mm = pe.matmul(ps[:, 0:n], zeros16[0:EP, 0:P], zeros16[0:EP, 0:n],
                               start=True, stop=False)
            mm.then_inc(s_sort_mm, SORT0)
            with pe.Fori(0, EC // SU) as i:
                for k in range(SU):
                    b, m = divmod(k, SB)
                    pe.wait_ge(s_hot, i * SU + (k + 1))
                    pe.wait_ge(s_ab, i * SU + (k + 1))
                    for ps, slot in ((sa_ps, slot_a), (sb_ps, slot_b)):
                        for half in range(2):
                            pe.matmul(ps[half][:, 0:HB], slot[:, m, :],
                                      tile_hot[:, k % SR, half * HB:(half + 1) * HB],
                                      start=False, stop=False)
                    pe.matmul(cnt_ps[:, 0:R * NW], node_hot[:, b, m, :], rw_hot[:, b, m, :],
                              start=False, stop=False).then_inc(s_sort_mm, 1)
            for ps, n in sums:
                mm = pe.matmul(ps[:, 0:n], zeros16[0:EP, 0:P], zeros16[0:EP, 0:n],
                               start=False, stop=True)
            mm.then_inc(s_sorted, 1)
            pe.wait_ge(s_inv, 1)
            pe.transpose(inv_ps[0:R * NW, 0:P], inv[:, :], ident[:, :]).then_inc(s_inv_t, 1)
            pe.wait_ge(s_dis, 1)

            aggregate(0, False)
            products(1, False)
            with pe.Fori(1, L) as q:
                aggregate(q)
                products(q + 1, False)
            aggregate(L)

        @block.scalar
        def _(act):
            act.sem_inc(s_xt, BUF)
            act.sem_inc(s_hev, BUF)
            def copy_transpose(hq, c, j):
                n = hq * NW + c * CW + j
                act.wait_ge(s_tp, n + 1)
                act.wait_ge(s_hmm, n + (BUF if j == 0 else BUF - 1))
                act.copy(xt[:, j % 2, :], xt_ps[j % 2][:, 0:D]).then_inc(s_xt, 1)

            def copy_products(hq, c, j, first):
                n = hq * NW + c * CW + j
                act.wait_ge(s_hmm, n + (BUF + 1))
                if first:
                    act.copy(cols(acc, c * CD + j * D, D), rel_ps[j % 2][0][:, 0:D]
                             ).then_inc(s_hev, 1)
                else:
                    act.wait_ge(s_hw[j], (hq * NC + c) * 16)
                    act.copy(hout[:, j, 0:2 * D], rel_ps[j % 2][0][:, :])
                    act.copy(hout[:, j, 2 * D:4 * D], rel_ps[j % 2][1][:, :]).then_inc(s_hev, 1)

            def copy_chunk(hq, c, first=False):
                copy_transpose(hq, c, 0)
                for j in range(CW):
                    if j + 1 < CW:
                        copy_transpose(hq, c, j + 1)
                    copy_products(hq, c, j, first)

            def copy_row_numbers(q, g, h, table):
                act.wait_ge(s_mm, q * NT + g * BODY + (MM0 - HALF + h * HALF))
                act.copy(idx[:, h * HALF:(h + 1) * HALF],
                         cols(table, g * BODY + h * HALF, HALF)).then_inc(s_idx, 1)

            def serve_messages(q):
                with act.Fori(0, NW) as g:
                    for h in range(2):
                        copy_row_numbers(q, g, h, g_rel)
                    act.copy(x_win[:, :], cols(X, g * D, D)).then_inc(s_xw, 1)
                    act.wait_ge(s_rt, (q - 1) * NW + g + 1)
                    act.copy(xt[:, 0, :], root_t_ps[:, 0:D]).then_inc(s_rx, 1)
                with act.Fori(NW, NG) as g:
                    for h in range(2):
                        copy_row_numbers(q, g, h, g_rel)

            def edge_matrices(t, k0, before, free):
                if free:
                    act.wait_ge(s_em, before * HALF)
                for i in range(HALF):
                    a = act.activation(square[:, i * P:(i + 1) * P], iota[:, 0:P], ACT.Square,
                                       bias=cols(neg_node, t + i, 1))
                a.then_inc(s_sq, 1)
                act.wait_ge(s_sq, before + 1)
                for i in range(HALF):
                    if free:
                        act.wait_ge(s_mm, t + (MM0 + i + 1 - BODY))
                    act.activation(emat[:, k0 + i, :], square[:, i * P:(i + 1) * P], ACT.Relu,
                                   bias=ones[:, 0:1], scale=-1.0).then_inc(s_em, 1)

            def root_of_variance(q):
                act.wait_ge(s_stat, q + 1)
                act.activation(sd[:, :], sd[:, :], ACT.Sqrt).then_inc(s_sd, 1)
                act.wait_ge(s_rstd, q + 1)

            def normalise(c, to):
                for j in range(CW):
                    a = act.activation(cols(to, c * CD + j * D, D), cols(acc, c * CD + j * D, D),
                                       ACT.Identity, bias=cols(nmr, c * CW + j, 1),
                                       scale=cols(rstd, c * CW + j, 1))
                a.then_inc(s_norm, 1)

            def exponentials(q, c):
                act.wait_ge(s_min, (q - 1) * NC + c + 1)
                act.activation(expo, expo, ACT.Exp).then_inc(s_exp, 1)

            with act.Fori(0, NC) as c:
                copy_chunk(0, c, True)
            with act.Fori(0, EC // SU) as i:
                for k in range(SU):
                    b, m = divmod(k, SB)
                    if m == 0:
                        act.wait_ge(s_lane, i * 2 + (b + 1))
                    act.wait_ge(s_sort_mm, i * SU + (SORT0 + k + 1 - SB))
                    for slot, val in ((slot_a, val_a), (slot_b, val_b)):
                        a = act.activation(slot[:, m, :], lane_hot[:, b, m, :], ACT.Copy,
                                           scale=val[:, bass.ds(i * SU + k, 1)])
                    a.then_inc(s_ab, 1)
            act.wait_ge(s_deg, 1)
            act.activation(deg_s[:, :], deg1[:, :], ACT.Sqrt).then_inc(s_degs, 1)
            act.wait_ge(s_dis, 1)

            def scale_rows(c, reused):
                for j in range(CW):
                    if reused:
                        act.wait_ge(s_hw[j], c * 16)
                    act.activation(hout[:, j, 0:D], cols(acc, c * CD + j * D, D), ACT.Copy,
                                   scale=cols(dis, c * CW + j, 1)).then_inc(s_h0, 1)

            scale_rows(0, False)
            with act.Fori(1, NC) as c:
                scale_rows(c, True)
            for j in range(CW):
                act.wait_ge(s_hw[j], 16 * NC)
            edge_matrices(0, 0, 0, False)
            with act.Fori(0, NG) as g:
                for h in range(2):
                    copy_row_numbers(0, g, h, g_src)
                    edge_matrices(g * BODY + (h + 1) * HALF, (1 - h) * HALF,
                                  g * 2 + (h + 1), True)
            root_of_variance(0)
            normalise(0, X)
            with act.Fori(1, NC) as c:
                normalise(c, X)
                copy_chunk(1, c - 1)
            copy_chunk(1, NC - 1)
            with act.Fori(1, L) as q:
                serve_messages(q)
                root_of_variance(q)
                normalise(0, acc)
                normalise(1, acc)
                exponentials(q, 0)
                with act.Fori(2, NC) as c:
                    normalise(c, acc)
                    exponentials(q, c - 1)
                    copy_chunk(q + 1, c - 2)
                exponentials(q, NC - 1)
                copy_chunk(q + 1, NC - 2)
                copy_chunk(q + 1, NC - 1)
            serve_messages(L)
            root_of_variance(L)
            normalise(0, acc)
            with act.Fori(1, NC) as c:
                normalise(c, acc)
                exponentials(L, c - 1)
            exponentials(L, NC - 1)
            root_of_variance(L + 1)
            with act.Fori(0, NC) as c:
                normalise(c, acc)

        @block.vector
        def _(dve):
            steps = [0]

            def done(ins, more=0):
                steps[0] += 1
                ins.then_inc(s_dve, 1)
                dve.wait_ge(s_dve, more + steps[0])

            dve.sem_inc(s_ra, 1)
            dve.wait_ge(s_edges, 48)
            dve.wait_ge(s_const, 1)
            done(dve.tensor_scalar(t1_i, dst_i, 7, None, ALU.arith_shift_right))
            dve.tensor_copy(d_hi, t1_i)
            done(dve.scalar_tensor_tensor(rel_win, typ_i, float(NW), t1_i, ALU.mult, ALU.add))
            done(dve.tensor_scalar(t1_i, dst_i, P - 1, None, ALU.bitwise_and))
            dve.tensor_copy(d_lo, t1_i)
            done(dve.tensor_scalar(t1_i, t1_i, 3, None, ALU.logical_shift_left))
            done(dve.tensor_scalar(t2_i, src_i, LOWBITS, None, ALU.arith_shift_right))
            done(dve.tensor_tensor(t1_i, t1_i, t2_i, ALU.bitwise_or))
            done(dve.tensor_scalar(val_b, t1_i, 1.0, None, ALU.add))
            done(dve.tensor_scalar(t2_i, src_i, LOW - 1, 2, ALU.bitwise_and,
                                   ALU.logical_shift_left))
            done(dve.tensor_tensor(t2_i, t2_i, typ_i, ALU.bitwise_or))
            done(dve.tensor_copy(val_a, t2_i))
            done(dve.memset(one_row, 1.0))
            with dve.Fori(0, NW) as w:
                c = dve.tensor_scalar(hit, d_hi, iota[0:EP, bass.ds(w, 1)], None,
                                      ALU.is_equal, ALU.add, accum_out=tot[0:EP, bass.ds(w, 1)])
                c.then_inc(s_dve, 1)
                dve.wait_ge(s_dve, w + (steps[0] + 1))
            steps[0] += NW
            done(dve.memset(pos, 0.0))
            dve.sem_inc(s_tot, 1)
            dve.wait_ge(s_base, 1)
            done(dve.tensor_scalar(n_tiles_i[:, :], misc_ps[:, 64:64 + NW], float(P - 1), None,
                                   ALU.add))
            done(dve.tensor_scalar(n_tiles_i[:, :], n_tiles_i[:, :], 7, None,
                                   ALU.arith_shift_right))
            done(dve.tensor_copy(n_tiles[:, :], n_tiles_i[:, :]))
            done(dve.tensor_tensor_scan(t_end[:, :], ones[:, 0:NW], n_tiles[:, :], 0.0,
                                        ALU.mult, ALU.add))
            done(dve.tensor_tensor(t_start[:, :], t_end[:, :], n_tiles[:, :], ALU.subtract))
            done(dve.scalar_tensor_tensor(run0[0:EP, :], t_start[0:EP, :], float(P),
                                          misc_ps[0:EP, 0:NW], ALU.mult, ALU.add))
            done(dve.tensor_scalar(run0[0:EP, :], run0[0:EP, :], -1.0, None, ALU.add))
            n0 = steps[0]
            with dve.Fori(0, NW) as w:
                steps[0] = n0
                m = w * 4
                done(dve.tensor_scalar(hit, d_hi, iota[0:EP, bass.ds(w, 1)], None,
                                       ALU.is_equal), m)
                done(dve.tensor_tensor_scan(run, one_row, hit, run0[0:EP, bass.ds(w, 1)],
                                            ALU.mult, ALU.add), m)
                done(dve.tensor_tensor(run, run, hit, ALU.mult), m)
                done(dve.tensor_tensor(pos, pos, run, ALU.add), m)
            steps[0] = n0 + 4 * NW
            done(dve.tensor_copy(t1_i, pos))
            done(dve.tensor_scalar(t2_i, t1_i, 7, None, ALU.arith_shift_right))
            done(dve.tensor_copy(pos_hi, t2_i))
            done(dve.tensor_scalar(t2_i, t1_i, P - 1, None, ALU.bitwise_and))
            done(dve.tensor_copy(pos_lo, t2_i))

            def spread(v, t, n):
                return (v[:, bass.ds(t, SB)].rearrange("p (s n) -> p s n", n=1)
                        .to_broadcast([EP, SB, n]))

            def lanes(n):
                return (iota16[0:EP, 0:n].rearrange("p (s n) -> p s n", s=1)
                        .to_broadcast([EP, SB, n]))

            with dve.Fori(0, EC // SU) as i:
                for b in range(2):
                    t = i * SU + b * SB
                    dve.wait_ge(s_sort_mm, i * SU + (SORT0 + b * SB - SB))
                    dve.tensor_tensor(lane_hot[:, b, :, :], lanes(P), spread(pos_lo, t, P),
                                      ALU.is_equal).then_inc(s_lane, 1)
                    dve.tensor_tensor(node_hot[:, b, :, :], lanes(P), spread(d_lo, t, P),
                                      ALU.is_equal)
                    dve.tensor_tensor(rw_hot[:, b, :, :], lanes(R * NW),
                                      spread(rel_win, t, R * NW), ALU.is_equal)
                    for m in range(SB):
                        k = b * SB + m
                        dve.wait_ge(s_sort_mm, i * SU + (SORT0 + k + 1 - SR))
                        dve.tensor_scalar(tile_hot[:, k % SR, :], iota16[0:EP, :],
                                          pos_hi[:, bass.ds(t + m, 1)], None,
                                          ALU.is_equal).then_inc(s_hot, 1)
            dve.wait_ge(s_sorted, 1)
            done(dve.tensor_copy(cnt[:, :], cnt_ps[:, 0:R * NW]))
            done(dve.tensor_scalar(inv[:, :], cnt[:, :], 1.0, None, ALU.max))
            dve.reciprocal(inv[:, :], inv[:, :]).then_inc(s_inv, 1)
            done(dve.tensor_reduce(deg[:, :], cnt[:, :].rearrange("p (r w) -> p w r", r=R),
                                   AXX, ALU.add))
            dve.tensor_scalar(deg1[:, :], deg[:, :], 1.0, None, ALU.max).then_inc(s_deg, 1)
            for b in range(2):
                half = slice(b * HB, (b + 1) * HB)
                dve.tensor_copy(a_i[:, half], sa_ps[b][:, 0:HB])
                dve.tensor_scalar(b_i[:, half], sb_ps[b][:, 0:HB], -1.0, None, ALU.add)
                done(dve.tensor_scalar(c_i[:, half], sb_ps[b][:, 0:HB], -1.0, 0.0, ALU.add,
                                       ALU.max))
            done(dve.tensor_scalar(b_i, b_i, 3, None, ALU.arith_shift_right))
            done(dve.memset(node[:, NT:MT], -1.0))
            done(dve.memset(weight[:, NT:MT], 0.0))
            done(dve.tensor_copy(node[:, 0:NT], b_i))
            done(dve.tensor_scalar(neg_node[:, :], node[:, :], -1.0, None, ALU.mult))
            done(dve.tensor_scalar(c_i, c_i, 7, LOWBITS, ALU.bitwise_and,
                                   ALU.logical_shift_left))
            done(dve.tensor_scalar(b_i, a_i, 2, None, ALU.arith_shift_right))
            done(dve.tensor_tensor(g_src[:, :], b_i, c_i, ALU.bitwise_or))
            done(dve.tensor_scalar(a_i, a_i, 3, None, ALU.bitwise_and))
            dve.scalar_tensor_tensor(g_rel[:, :], a_i, float(NPAD), g_src[:, :],
                                     ALU.mult, ALU.add)
            done(dve.scalar_tensor_tensor(key[:, :], a_i, float(P), node[:, 0:NT],
                                          ALU.mult, ALU.add))
            dve.wait_ge(s_inv_t, 1)
            dve.tensor_copy(inv_t[:, :], inv_ps[0:R * NW, 0:P]).then_inc(s_inv_s, 1)
            dve.wait_ge(s_degs, 1)
            done(dve.reciprocal(deg_s[:, :], deg_s[:, :]))
            dve.scalar_tensor_tensor(dis[:, :], deg[:, :], 0.0, deg_s[:, :],
                                     ALU.is_gt, ALU.mult).then_inc(s_dis, 1)
            done(dve.memset(win_f[:, :], -1.0))
            with dve.Fori(0, NW) as w:
                dve.scalar_tensor_tensor(win_f[:, :], iota16[:, :], t_start[:, bass.ds(w, 1)],
                                         win_f[:, :], ALU.is_ge, ALU.add).then_inc(s_dve, 1)
                dve.wait_ge(s_dve, w + (steps[0] + 1))
            steps[0] += NW
            done(dve.tensor_copy(win_i[:, :], win_f[0:1, :]))
            dve.wait_ge(s_h0, NW)
            dve.memset(acc, 0.0).then_inc(s_acc, ACC0)

            def edge_matrix(t, k, free):
                if free is not None:
                    dve.wait_ge(s_mm, free)
                dve.tensor_scalar(emat[:, k % BODY, :], iota[:, 0:P], cols(node, t, 1),
                                  cols(weight, t, 1), ALU.is_equal, ALU.mult
                                  ).then_inc(s_em, 1)

            inv_v = inv_b.rearrange("p (r w d) -> p r w d", r=R, w=NW)
            key_v = iota[:, :].rearrange("p (r d) -> p r d", r=R)

            def add_tiles(q, g, first, root):
                for h in range(2):
                    _, wins = nc.values_load_multi_w_load_instructions(
                        win_i[0:1, bass.ds(g * BODY + h * HALF, HALF)],
                        engines=[mybir.EngineType.DVE], min_val=0, max_val=NW - 1,
                        skip_runtime_bounds_check_because="a tile's window is below NW")
                    for i in range(HALF):
                        k = h * HALF + i
                        t = g * BODY + k
                        if first:
                            dve.scalar_tensor_tensor(
                                found[:, k % 2, :, :], key_v, cols(key, t, 1),
                                inv_v[:, :, bass.ds(wins[i], 1), :]
                                .rearrange("p r w d -> p r (w d)"),
                                ALU.is_equal, ALU.mult, accum_out=cols(weight, t, 1))
                        else:
                            edge_matrix(t + HALF, k + HALF,
                                        q * NT + g * BODY + (MM0 + k + HALF + 1 - BODY))
                        dve.wait_ge(s_mm, q * NT + g * BODY + (MM0 + k + 1))
                        dve.wait_ge(s_acc, q * NT + g * BODY + (ACC0 + k))
                        a = cols(acc, wins[i] * D, D)
                        dve.tensor_tensor(a, a, agg_ps[k % NPS][:, 0:D], ALU.add
                                          ).then_inc(s_acc, 1)
                        if root and k == 16:
                            dve.wait_ge(s_rm, (q - 1) * NW + g + 1)
                            dve.wait_ge(s_acc, q * NT + g * BODY + (ACC0 + k + 1))
                            a = cols(acc, g * D, D)
                            dve.tensor_tensor(a, a, root_ps[:, 0:D], ALU.add
                                              ).then_inc(s_ra, 1)
                            dve.wait_ge(s_ra, (q - 1) * NW + g + 2)

            def messages(q, first):
                if first:
                    dve.wait_ge(s_inv_b, 16)
                    with dve.Fori(0, NG) as g:
                        add_tiles(q, g, True, False)
                else:
                    for k in range(HALF):
                        edge_matrix(k, k, None)
                    dve.wait_ge(s_zero, q * NC)
                    apart(dve)
                    with dve.Fori(0, NW) as g:
                        add_tiles(q, g, False, True)
                    with dve.Fori(NW, NG) as g:
                        add_tiles(q, g, False, False)

            def statistics(w, more):
                done(dve.bn_stats(stats[:, bass.ds(w, 1), :].rearrange("p w s -> p (w s)"),
                                  cols(acc, w * D, D)), more)

            def scales(q, more):
                mean_e, dev_e, mean_o, dev_o = (stats[:, :, k] for k in (1, 2, 4, 5))
                done(dve.tensor_tensor(mean[:, :], mean_e, mean_o, ALU.add), more)
                done(dve.tensor_scalar(mean[:, :], mean[:, :], 0.5, None, ALU.mult), more)
                done(dve.tensor_tensor(gap[:, :], mean_e, mean_o, ALU.subtract), more)
                done(dve.scalar_tensor_tensor(gap[:, :], gap[:, :], 0.25, gap[:, :],
                                              ALU.mult, ALU.mult), more)
                done(dve.tensor_tensor(sd[:, :], dev_e, dev_o, ALU.add), more)
                done(dve.scalar_tensor_tensor(sd[:, :], sd[:, :], 1.0 / D, gap[:, :],
                                              ALU.mult, ALU.add), more)
                dve.tensor_scalar(sd[:, :], sd[:, :], EPS, None, ALU.add).then_inc(s_stat, 1)
                dve.wait_ge(s_sd, q + 1)
                done(dve.reciprocal(rstd[:, :], sd[:, :]), more)
                dve.scalar_tensor_tensor(nmr[:, :], mean[:, :], -1.0, rstd[:, :],
                                         ALU.mult, ALU.mult).then_inc(s_rstd, 1)

            messages(0, True)
            dve.wait_ge(s_acc, ACC0 + NT)
            n0 = steps[0]
            with dve.Fori(0, NW) as w:
                steps[0] = n0
                done(dve.scalar_tensor_tensor(cols(acc, w * D, D), cols(acc, w * D, D),
                                              cols(dis, w, 1), cols(X, w * D, D),
                                              ALU.mult, ALU.add), w * 2)
                statistics(w, w * 2)
            steps[0] = n0 + 2 * NW
            scales(0, 0)
            with dve.Fori(0, NC) as c:
                dve.wait_ge(s_norm, c + 1)
                dve.tensor_copy(cols(X1, c * CD, CD), cols(X, c * CD, CD)).then_inc(s_xr, 1)

            def relational(q, more, last=False):
                messages(q, False)
                dve.wait_ge(s_acc, q * NT + (ACC0 + NT))
                apart(dve)
                n = steps[0]
                with dve.Fori(0, NW) as w:
                    steps[0] = n
                    statistics(w, w + more)
                steps[0] = n + NW
                scales(q, more)
                dve.wait_ge(s_gb, q * 32)
                apart(dve)
                n = steps[0]
                with dve.Fori(0, NC) as c:
                    steps[0] = n
                    m = c * 3 + more
                    y = cols(acc, c * CD, CD)
                    y3 = y.rearrange("p (w d) -> p w d", w=CW)
                    xc = cols(X, c * CD, CD)
                    dve.wait_ge(s_norm, q * NC + c + 1)
                    for v, op in ((gamma_sb, ALU.mult), (beta_sb, ALU.add)):
                        done(dve.tensor_tensor(y3, y3, v[:, :].rearrange("p (w d) -> p w d", w=1)
                                               .to_broadcast([P, CW, D]), op), m)
                    dve.tensor_scalar(expo, y, 0.0, None, ALU.min).then_inc(s_min, 1)
                    dve.wait_ge(s_exp, (q - 1) * NC + c + 1)
                    done(dve.scalar_tensor_tensor(y, y, 0.0, expo, ALU.max, ALU.add), m)
                    dve.scalar_tensor_tensor(xc, y, -1.0, xc, ALU.add, ALU.add
                                             ).then_inc(s_xr, 1)
                    if last:
                        dve.wait_ge(s_xr, q * NC + c + 1)
                        dve.tensor_tensor(y, xc, cols(X1, c * CD, CD), ALU.add
                                          ).then_inc(s_final, 1)
                        dve.wait_ge(s_final, c * (CW + 1) + 1)
                        for j in range(CW):
                            dve.bn_stats(stats[:, bass.ds(c * CW + j, 1), :]
                                         .rearrange("p w s -> p (w s)"),
                                         cols(acc, c * CD + j * D, D)).then_inc(s_final, 1)
                        dve.wait_ge(s_final, c * (CW + 1) + (CW + 1))
                steps[0] = n + 3 * NC

            n0 = steps[0]
            per_layer = NW + 7 + 3 * NC
            with dve.Fori(1, L) as q:
                steps[0] = n0
                relational(q, (q - 1) * per_layer)
                assert steps[0] == n0 + per_layer
            steps[0] = n0 + (L - 1) * per_layer
            relational(L, 0, last=True)
            scales(L + 1, 0)


_INS = ['x', 'src', 'dst', 'edge_type_4', 'L0_gnn_W', 'L1_gnn_weights', 'L1_gnn_roots',
        'L1_gnn_biases', 'L1_gnn_ln_gamma', 'L1_gnn_ln_beta']


def kernel(**inputs):
    import numpy as _np
    import concourse.bacc as _bacc
    from concourse.bass_utils import run_bass_kernel_spmd as _run

    f32 = mybir.dt.float32
    nc = _bacc.Bacc("TRN2", target_bir_lowering=False, num_devices=1)
    arrays, args = {}, []
    for name in _INS:
        a = _np.ascontiguousarray(inputs[name])
        arrays[f"in_{name}_dram"] = a
        args.append(nc.dram_tensor(f"in_{name}_dram", a.shape, mybir.dt.from_np(a.dtype),
                                   kind="ExternalInput").ap())
    n, d = inputs['x'].shape
    r = inputs['L1_gnn_weights'].shape[1]
    rows = -(-n // 128) * 128
    out = nc.dram_tensor("out_0_dram", (n, d), f32, kind="ExternalOutput").ap()
    h0_table = nc.dram_tensor("h0_table", (rows, d), f32, kind="Internal").ap()
    h_table = nc.dram_tensor("h_table", (r * rows, d), f32, kind="Internal").ap()
    inv_dram = nc.dram_tensor("inv_dram", (r * rows // 128, 128), f32, kind="Internal").ap()
    build_program(nc, *args, out, h0_table, h_table, inv_dram)
    res = _run(nc, [arrays], core_ids=[0])
    return res.results[0]["out_0_dram"]
```

```python
import concourse.bass as bass
from concourse import mybir
from contextlib import ExitStack


def build_program(nc, x, src, dst, etype, w0, weights, roots, biases, gammas, betas, out,
                  h0_table, h_tables, inv_dram, x1_dram, placed_dram):
    f32, f16, i32 = mybir.dt.float32, mybir.dt.float16, mybir.dt.int32
    ALU = mybir.AluOpType
    ACT = mybir.ActivationFunctionType
    AXX = mybir.AxisListType.X

    N, D = x.shape
    E = src.shape[0]
    L, R = weights.shape[0], weights.shape[1]
    P = 128
    NW = -(-N // P)
    TAIL = N - (NW - 1) * P
    NPAD = NW * P
    KT = D // P
    EP = 125
    EC = E // EP
    assert EP * EC == E
    NT = (E + NW * (P - 1)) // P
    HALF = 16
    BODY = 2 * HALF
    NB = NT // BODY
    REST = NT - NB * BODY
    assert NB == NW and 0 < REST < HALF
    QT = HALF // 2
    MT = NB * BODY + 2 * HALF
    ME = NB * BODY + HALF
    NI = NB * BODY + 3 * QT
    RING = HALF
    assert all(j * NT // NW <= j * BODY + REST for j in range(NW))
    NPS = 4
    SB = 8
    SU = 2 * SB
    SM = SB // 2
    SS = SB - SM
    SR = 2 * SM
    HB = NT // 2
    assert HB * 2 == NT and HB <= 512 and EC % SU == 0
    CW = 5
    NC = NW // CW
    SLOT = (0, 1, 0, 1, 2)
    CD = CW * D
    EPS = 1e-5
    LOWBITS = 9
    LOW = 1 << LOWBITS

    ctx = ExitStack()
    with ctx:
        def sb(name, shape, dt=f32):
            return ctx.enter_context(nc.sbuf_tensor(name, shape, dt))

        def sem(name):
            return ctx.enter_context(nc.semaphore(name))

        ident = sb("ident", [P, P])
        ones = sb("ones", [P, P])
        before = sb("before", [EP, EP])
        iota = sb("iota", [P, R * P])
        iota16 = sb("iota16", [P, NT], f16)
        zeros16 = sb("zeros16", [P, 512], f16)
        g_src = sb("g_src", [P, NI], i32)
        g_rel = sb("g_rel", [P, NI], i32)
        node = sb("node", [P, MT])
        key = sb("key", [P, NT])
        weight = sb("weight", [P, MT])
        win_i = sb("win_i", [1, NT], i32)
        order_i = sb("order_i", [1, NW], i32)
        dis = sb("dis", [P, NW])
        X = sb("X", [P, NW * D])
        arena = sb("arena", [P, 12800 + 6400])
        X1 = arena[:, 0:NW * D]
        acc = arena[:, 12800:12800 + NW * D]
        inv_b = arena[:, 0:R * NPAD]
        msg = sb("msg", [P, RING, D])
        idx = sb("idx", [P, BODY], i32)
        emat = sb("emat", [P, BODY, P])
        found = sb("found", [P, 2, R, P], f16)
        w0_sb = sb("w0_sb", [P, KT, D])
        w_sb = sb("w_sb", [P, KT, R, D])
        root_sb = sb("root_sb", [P, KT, D])
        bias_sb = sb("bias_sb", [1, D])
        gamma_sb = sb("gamma_sb", [P, D])
        beta_sb = sb("beta_sb", [P, D])
        xt = sb("xt", [P, 3, D])
        hout = sb("hout", [P, CW, R * D])
        eps_col = sb("eps_col", [P, 1])
        wstats = sb("wstats", [P, 6])
        wmv = sb("wmv", [P, 2])
        wsd = sb("wsd", [P, 1])
        wrstd = sb("wrstd", [P, 1])
        wnmr = sb("wnmr", [P, 1])
        neg_node = sb("neg_node", [P, MT])
        square = hout[:, 1:3, :].rearrange("p a b -> p (a b)")
        assert HALF * P == 2 * R * D
        y_win, e_win, x_win = (hout[:, 3, k * D:(k + 1) * D] for k in range(3))
        at = [0]

        def tmp(cols, dt=f32):
            a = arena[0:EP, at[0]:at[0] + cols]
            at[0] += cols
            return a if dt is f32 else a.bitcast(dt)

        src_i, dst_i, typ_i = tmp(EC, i32), tmp(EC, i32), tmp(EC, i32)
        t1_i, t2_i = tmp(EC, i32), tmp(EC, i32)
        hits = (src_i.bitcast(f16)[:, 0:EC], src_i.bitcast(f16)[:, EC:2 * EC],
                tmp(EC // 2, f16))
        runs = (dst_i.bitcast(f32), t2_i.bitcast(f32), tmp(EC))
        one_row = typ_i.bitcast(f32)
        EX = EC + SB
        d_hi, record, pos = tmp(EC // 2, f16), tmp(2 * EC), tmp(EC)
        record = record.rearrange("p (c v) -> p c v", v=2)
        val_a, val_b = record[:, :, 0], record[:, :, 1]
        row = pos.bitcast(i32)
        d_lo, rel_win, pos_hi, pos_lo = tmp(EX), tmp(EX), tmp(EC), tmp(EX)
        rw_hot = tmp(SU * R * NW // 2, f16).rearrange("p (b s n) -> p b s n", b=2, s=SB)
        assert at[0] <= 12800
        tile_hot = (arena[0:EP, 0:SR * NT // 2].bitcast(f16)
                    .rearrange("p (s n) -> p s n", s=SR))
        assert SR * NT // 2 <= 5 * EC
        cells = emat[0:EP, :, :].rearrange("p a b -> p (a b)").bitcast(f16)
        batch = SB * P
        lane_hot, node_hot = (cells[:, k * 2 * batch:(k + 1) * 2 * batch]
                              .rearrange("p (b s n) -> p b s n", b=2, s=SB) for k in range(2))
        slot_a, slot_b = (cells[:, (4 + k) * batch:(5 + k) * batch]
                          .rearrange("p (s n) -> p s n", s=SB) for k in range(2))
        flat = emat[:, :, :].rearrange("p a b -> p (a b)")
        placed = flat[:, 0:2 * NT].rearrange("p (t v) -> p t v", v=2)
        assert 3 * NT <= BODY * P
        win_ge = flat[0:NW, 2 * NT:3 * NT]
        a_i = msg[:, 0:4, :].rearrange("p a b -> p (a b)")[:, 0:NT].bitcast(i32)
        b_i = msg[:, 4:8, :].rearrange("p a b -> p (a b)")[:, 0:NT].bitcast(i32)
        c_i = msg[:, 8:12, :].rearrange("p a b -> p (a b)")[:, 0:NT].bitcast(i32)
        tot = sb("tot", [P, NW])
        n_tiles_i = sb("n_tiles_i", [P, NW], i32)
        n_tiles = sb("n_tiles", [P, NW])
        size_key = sb("size_key", [P, NW])
        place = sb("place", [P, NW])
        order = sb("order", [P, NW])
        order_step = sb("order_step", [P, NW])
        leaving = sb("leaving", [EP, 2 * SS, 2])
        pick = sb("pick", [NW, NW])
        order_col = sb("order_col", [NW, 1])
        first_col = sb("first_col", [NW, 1])
        t_start = sb("t_start", [P, NW])
        t_first = sb("t_first", [P, NW])
        pair_a, pair_b = (msg[:, 4 * k:4 * k + 3, :].rearrange("p a b -> p (a b)")[:, 0:NW * NW]
                          .rearrange("p (w v) -> p w v", w=NW) for k in range(2))
        run0 = sb("run0", [P, NW])
        cnt = sb("cnt", [P, R * NW])
        inv = sb("inv", [P, R * NW])
        inv_t = sb("inv_t", [R * NW, P])
        deg = sb("deg", [P, NW])
        deg1 = sb("deg1", [P, NW])
        deg_s = sb("deg_s", [P, NW])

        banks = [ctx.enter_context(nc.psum_tensor(f"bank{i}", [P, 512], f32)) for i in range(8)]
        agg_ps = banks[0:NPS]
        xt_ps = banks[0:2]
        win_t_ps, root_ps, win_ps = banks[4], banks[5], banks[6:8]
        w0_ps = (banks[2], banks[3], banks[4])
        sa_ps, sb_ps, cnt_ps, misc_ps, inv_ps = banks[0:2], banks[2:4], banks[4], banks[5], banks[6]

        s_edges = sem("s_edges")
        s_x = sem("s_x")
        s_w0 = sem("s_w0")
        s_w = sem("s_w")
        s_root = sem("s_root")
        s_gb = sem("s_gb")
        s_const = sem("s_const")
        s_pool = sem("s_pool")
        s_dve = sem("s_dve")
        s_tot = sem("s_tot")
        s_base = sem("s_base")
        s_hot = sem("s_hot")
        s_sort_mm = sem("s_sort_mm")
        s_sorted = sem("s_sorted")
        s_inv = sem("s_inv")
        s_inv_t = sem("s_inv_t")
        s_inv_s = sem("s_inv_s")
        s_inv_w = sem("s_inv_w")
        s_inv_b = sem("s_inv_b")
        s_deg = sem("s_deg")
        s_degs = sem("s_degs")
        s_dis = sem("s_dis")
        s_xpad = sem("s_xpad")
        s_tp = sem("s_tp")
        s_xt = sem("s_xt")
        s_hmm = sem("s_hmm")
        s_hev = sem("s_hev")
        s_hw = [sem(f"s_hw{j}") for j in range(CW)]
        s_idx = sem("s_idx")
        s_msg = [sem(f"s_msg{k}") for k in range(RING)]
        s_em = sem("s_em")
        s_mm = sem("s_mm")
        s_acc = sem("s_acc")
        s_min = sem("s_min")
        s_exp = sem("s_exp")
        s_apart = sem("s_apart")
        s_h0 = sem("s_h0")
        s_lane = sem("s_lane")
        s_ab = sem("s_ab")
        s_sq = sem("s_sq")
        s_first = sem("s_first")
        s_nmr = sem("s_nmr")
        s_x1w = sem("s_x1w")
        s_x1 = sem("s_x1")
        s_step = sem("s_step")
        s_var = sem("s_var")
        s_wsd = sem("s_wsd")
        s_xn = sem("s_xn")
        s_xc = sem("s_xc")
        s_tw = sem("s_tw")
        s_xe = sem("s_xe")
        s_hm = sem("s_hm")
        s_ev = sem("s_ev")
        s_hs = sem("s_hs")
        s_fin = sem("s_fin")
        s_fsd = sem("s_fsd")
        s_pos0 = sem("s_pos0")
        s_rank = sem("s_rank")
        s_ranked = sem("s_ranked")
        s_wcol = sem("s_wcol")
        s_wmm = sem("s_wmm")
        s_clear = sem("s_clear")
        s_cleared = sem("s_cleared")
        s_rows = sem("s_rows")
        s_scat = [sem(f"s_scat{b}") for b in range(2)]
        s_back = sem("s_back")
        s_win = sem("s_win")
        s_decoded = sem("s_decoded")
        s_outn = sem("s_outn")
        s_out = sem("s_out")

        MM0 = BODY
        ACC0 = NPS
        BUF = 2
        SORT0 = SU
        ONE0 = 1
        NFIRST, NSTEP, NFIN = 3, 5, 5
        QUARTERS = 4 * NB + 3

        def matrices_before(q):
            return q * ME + (HALF if q else 0)

        block = ctx.enter_context(nc.Block())

        def cols(tensor, start, n):
            return tensor[:, bass.ds(start, n)]

        def window_at(eng, j):
            return nc.values_load_multi_w_load_instructions(
                order_i[0:1, bass.ds(j, 1)], engines=[eng], min_val=0, max_val=NW - 1,
                skip_runtime_bounds_check_because="a window's number is below NW")[1][0]

        def apart(eng):
            eng.sem_inc(s_apart, 1)

        @block.sync
        def _(sp):
            for lst, at_ in ((src, src_i), (dst, dst_i), (etype, typ_i)):
                sp.dma_start(at_, lst.rearrange("(p t) -> p t", p=EP)).then_inc(s_edges, 16)
            xv = X[:, :].rearrange("p (w d) -> p w d", w=NW)
            sp.dma_start(xv[:, 0:NW - 1, :],
                         x[0:(NW - 1) * P, :].rearrange("(w p) d -> p w d", p=P)).then_inc(s_x, 16)
            sp.wait_ge(s_xpad, 1)
            sp.dma_start(xv[0:TAIL, NW - 1, :], x[(NW - 1) * P:N, :]).then_inc(s_x, 16)
            sp.dma_start(w0_sb[:, :, :], w0.rearrange("(k p) o -> p k o", p=P)).then_inc(s_w0, 16)

            placed_rows = placed_dram.rearrange("(p t) v -> p t v", p=P)
            sp.wait_ge(s_clear, 1)
            sp.dma_start(placed_rows, placed).then_inc(s_cleared, 16)

            def load_weights(l):
                for k in range(KT):
                    sp.dma_start(w_sb[:, k, :, :],
                                 weights[bass.ds(l, 1), :, k * P:(k + 1) * P, :]
                                 .rearrange("l r p o -> p (l r) o")).then_inc(s_w, 16)

            def load_root(l):
                sp.dma_start(root_sb[:, :, :],
                             roots[bass.ds(l, 1), :, :].rearrange("l (k p) o -> p (l k) o", p=P)
                             ).then_inc(s_root, 16)
                sp.dma_start(bias_sb[:, :], biases[bass.ds(l, 1), :]).then_inc(s_root, 16)

            def load_affine(l):
                for v, to in ((gammas, gamma_sb), (betas, beta_sb)):
                    sp.dma_start(to[:, :], v[bass.ds(l, 1), :].to_broadcast([P, D])
                                 ).then_inc(s_gb, 16)

            load_weights(0)
            load_root(0)
            load_affine(0)
            h0_view = h0_table.rearrange("(w p) o -> w p o", p=P)
            x1_view = x1_dram.rearrange("(w p) d -> w p d", p=P)
            h_views = [h.rearrange("(r w p) o -> w p r o", r=R, p=P) for h in h_tables]

            for b in range(2):
                sp.wait_ge(s_scat[b], EC // SU * (16 * SS))
            sp.wait_ge(s_sorted, 1)
            sp.dma_start(placed, placed_rows).then_inc(s_back, 16)
            with sp.Fori(0, NC) as c:
                for j in range(CW):
                    sp.wait_ge(s_h0, c * CW + (j + 1))
                    sp.dma_start(h0_view[bass.ds(c * CW + j, 1), :, :]
                                 .rearrange("w p o -> (w p) o"),
                                 hout[:, j, 0:D]).then_inc(s_hw[j], 16)
            sp.wait_ge(s_inv_s, 1)
            sp.dma_start(inv_dram[:, :], inv_t[:, :]).then_inc(s_inv_w, 16)
            sp.wait_ge(s_inv_w, 16)
            sp.dma_start(inv_b, inv_dram.rearrange("(a r) d -> a (r d)", a=1)
                         .to_broadcast([P, R * NPAD])).then_inc(s_inv_b, 16)
            for q in range(L + 1):
                if q > 0:
                    sp.wait_ge(s_hm, q * NW)
                    if q < L:
                        load_weights(q)
                        load_root(q)
                    if q > 1:
                        load_affine(q - 1)
                if q == 1:
                    sp.wait_ge(s_x1w, (NW + ONE0) * 16)
                    sp.dma_start(X1.rearrange("p (w d) -> p w d", w=NW),
                                 x1_dram.rearrange("(w p) d -> p w d", p=P)).then_inc(s_x1, 16)
                if q < L:
                    with sp.Fori(0, NW) as j:
                        v = window_at(mybir.EngineType.SP, j)
                        if q == 0:
                            sp.wait_ge(s_xn, j + 1)
                            sp.dma_start(x1_view[bass.ds(v, 1), :, :]
                                         .rearrange("w p d -> (w p) d"),
                                         x_win).then_inc(s_x1w, 16)
                        sp.wait_ge(s_ev, j + (q * NW + ONE0 + 1))
                        sp.dma_start(h_views[(q + 1) % 2][bass.ds(v, 1), :, :, :]
                                     .rearrange("w p r o -> (w p) r o"),
                                     hout[:, 0, :].rearrange("p (r o) -> p r o", r=R)
                                     ).then_inc(s_hs, 16)
            ov = acc.rearrange("p (w d) -> p w d", w=NW)
            sp.wait_ge(s_outn, NW)
            for c in range(NC):
                w0_, w1 = c * CW, min((c + 1) * CW, NW - 1)
                sp.dma_start(out[w0_ * P:w1 * P, :].rearrange("(w p) d -> p w d", p=P),
                             ov[:, w0_:w1, :]).then_inc(s_out, 16)
            sp.dma_start(out[(NW - 1) * P:N, :], ov[0:TAIL, NW - 1, :]).then_inc(s_out, 16)
            sp.wait_ge(s_out, (NC + 1) * 16)

        @block.gpsimd
        def _(pool):
            pool.memset(X[:, (NW - 1) * D:NW * D], 0.0).then_inc(s_xpad, 1)
            pool.iota(iota[:, :], [[1, R * P]], base=0, channel_multiplier=0,
                      allow_small_or_imprecise_dtypes=True)
            pool.iota(iota16[:, :], [[1, NT]], base=0, channel_multiplier=0,
                      allow_small_or_imprecise_dtypes=True)
            pool.memset(zeros16[:, :], 0.0)
            pool.memset(eps_col[:, :], EPS)
            pool.memset(ones[:, :], 1.0)
            pool.memset(before[:, :], 1.0).then_inc(s_pool, 1)
            pool.memset(ident[:, :], 0.0).then_inc(s_pool, 1)
            pool.wait_ge(s_pool, 1)
            pool.affine_select(out=before[:, :], in_=before[:, :], compare_op=ALU.is_gt, fill=0.0,
                               base=0, pattern=[[1, EP]], channel_multiplier=-1)
            pool.wait_ge(s_pool, 2)
            pool.affine_select(out=ident[:, :], in_=ident[:, :], compare_op=ALU.not_equal,
                               fill=1.0, base=0, pattern=[[-1, P]], channel_multiplier=1
                               ).then_inc(s_const, 1)

            pool.memset(flat[:, 0:2 * NT], 0.0).then_inc(s_clear, 1)

            pool.wait_ge(s_pos0, 1)
            pool.sem_inc(s_ranked, BUF)
            with pool.Fori(0, NW // CW) as i:
                for j in range(CW):
                    pool.wait_ge(s_rank, i * CW + (j + 2))
                    pool.wait_ge(s_ranked, i * CW + (BUF + j))
                    pool.tensor_tensor(pos, pos, runs[SLOT[j]], ALU.add).then_inc(s_ranked, 1)
            pool.wait_ge(s_cleared, 16)
            with pool.Fori(0, EC // SU) as i:
                for b in range(2):
                    pool.wait_ge(s_rows, i * 2 + (b + 1))
                    apart(pool)
                    for m in range(SS):
                        n = b * SS + m
                        pool.indirect_dma_start(
                            out=placed_dram[:, :],
                            out_offset=bass.IndirectOffsetOnAxis(ap=idx[0:EP, n:n + 1], axis=0),
                            in_=leaving[:, n, :],
                            in_offset=None).then_inc(s_scat[b], 16)

            def gather_tiles(q, g, n, table):
                for k in range(n):
                    if k % QT == 0:
                        pool.wait_ge(s_idx, g * 4 + (q * QUARTERS + k // QT + 1))
                    pool.wait_ge(s_mm, g * BODY + (q * NT + MM0 + k + 1 - RING))
                    apart(pool)
                    pool.indirect_dma_start(
                        out=msg[:, k % RING, :], out_offset=None, in_=table[:, :],
                        in_offset=bass.IndirectOffsetOnAxis(ap=idx[:, k:k + 1], axis=0)
                    ).then_inc(s_msg[k % RING], 16)

            def gather(q, table):
                if q == 0:
                    for j in range(CW):
                        pool.wait_ge(s_hw[j], 16 * NC)
                else:
                    pool.wait_ge(s_hs, (q * NW + ONE0) * 16)
                with pool.Fori(0, NB) as g:
                    gather_tiles(q, g, BODY, table)
                gather_tiles(q, NB, REST, table)

            gather(0, h0_table)
            for q in range(1, L + 1):
                gather(q, h_tables[q % 2])

        @block.tensor
        def _(pe):
            pe.wait_ge(s_const, 1)
            pe.sem_inc(s_hmm, BUF)

            def transpose_window(w):
                c, j = divmod(w, CW)
                pe.wait_ge(s_xt, w + (BUF if j == 0 else BUF - 1))
                for k in range(KT):
                    tp = pe.transpose(xt_ps[j % 2][:, k * P:(k + 1) * P],
                                      X[:, w * D + k * P:w * D + (k + 1) * P], ident[:, :])
                tp.then_inc(s_tp, 1)

            def multiply_window(w):
                s = SLOT[w % CW]
                pe.wait_ge(s_xt, w + BUF + 1)
                pe.wait_ge(s_hev, w + BUF - 1)
                for k in range(KT):
                    mm = pe.matmul(w0_ps[s][:, 0:D], xt[:, s, k * P:(k + 1) * P],
                                   w0_sb[:, k, :], start=(k == 0), stop=(k == KT - 1))
                mm.then_inc(s_hmm, 1)

            def edge_sums():
                pe.wait_ge(s_tot, 1)
                pe.matmul(misc_ps[0:EP, 0:NW], before[:, :], tot[0:EP, :], start=True, stop=True
                          ).then_inc(s_mm, MM0)
                pe.matmul(misc_ps[:, 64:64 + NW], ones[0:EP, :], tot[0:EP, :],
                          start=True, stop=True).then_inc(s_base, 1)

            def first_products():
                pe.wait_ge(s_x, 32)
                pe.wait_ge(s_w0, 16)
                transpose_window(0)
                for w in range(NW):
                    if w == NW // 2:
                        edge_sums()
                    if w + 1 < NW:
                        transpose_window(w + 1)
                    multiply_window(w)

            def window_transposed(q, n):
                pe.wait_ge(s_xn, n + 1)
                pe.wait_ge(s_xe, n + ONE0)
                for k in range(KT):
                    tp = pe.transpose(win_t_ps[:, k * P:(k + 1) * P],
                                      x_win[:, k * P:(k + 1) * P], ident[:, :])
                tp.then_inc(s_tw, 1)

            def window_product(q, n, h, k):
                if h == 0 and k == 0:
                    pe.wait_ge(s_xe, n + (ONE0 + 1))
                    pe.wait_ge(s_ev, n + ONE0)
                    pe.wait_ge(s_w, (q + 1) * (16 * KT))
                pe.matmul(win_ps[h][:, :], xt[:, 0, k * P:(k + 1) * P],
                          w_sb[:, k, 2 * h:2 * h + 2, :].rearrange("p r o -> p (r o)"),
                          start=(k == 0), stop=(k == KT - 1))

            def window_root(q, n, k):
                if k == 0:
                    pe.wait_ge(s_root, (q + 1) * 32)
                pe.matmul(root_ps[:, 0:D], xt[:, 0, k * P:(k + 1) * P], root_sb[:, k, :],
                          start=(k == 0), stop=False)
                if k == KT - 1:
                    pe.matmul(root_ps[:, 0:D], ones[0:1, :], bias_sb[:, :],
                              start=False, stop=True).then_inc(s_hm, 1)

            def window_work(q, n):
                at0 = 20 if q else 16
                work = {at0: lambda: window_transposed(q, n)}
                for i in range(2 * KT):
                    h, k = divmod(i, KT)
                    work[at0 + 3 + i] = lambda h=h, k=k: window_product(q, n, h, k)
                for k in range(KT):
                    work[at0 + 3 + 2 * KT + k] = lambda k=k: window_root(q, n, k)
                return work

            def tile_products(q, g, tiles, work):
                for k in range(tiles):
                    if k in work:
                        work[k]()
                    pe.wait_ge(s_em, g * BODY + (matrices_before(q) + k + 1))
                    per_pass = 2 * NB + (1 if k % RING < REST else 0)
                    pe.wait_ge(s_msg[k % RING], g * 32 + (q * per_pass + k // RING + 1) * 16)
                    pe.wait_ge(s_acc, g * BODY + (q * NT + ACC0 + k + 1 - NPS))
                    pe.matmul(agg_ps[k % NPS][:, 0:D], emat[:, k, :], msg[:, k % RING, :],
                              start=True, stop=True).then_inc(s_mm, 1)

            def aggregate(q):
                if q > 0:
                    pe.wait_ge(s_ev, q * NW + ONE0)
                tile_products(q, 0, BODY, {})
                with pe.Fori(1, NB) as g:
                    tile_products(q, g, BODY,
                                  window_work(q, g + (q * NW - 1)) if q < L else {})
                tile_products(q, NB, REST, {})
                if q < L:
                    for part in window_work(q, (q + 1) * NW - 1).values():
                        part()

            first_products()
            pe.wait_ge(s_wcol, 1)
            for half in range(2):
                mm = pe.matmul(banks[6 + half][0:1, 0:HB], order_col[:, :],
                               win_ge[:, half * HB:(half + 1) * HB], start=True, stop=True)
            mm.then_inc(s_wmm, 1)
            pe.wait_ge(s_hev, BUF + NW)
            sums = [(sa_ps[0], HB), (sa_ps[1], HB), (sb_ps[0], HB), (sb_ps[1], HB),
                    (cnt_ps, R * NW)]
            for ps, n in sums:
                mm = pe.matmul(ps[:, 0:n], zeros16[0:EP, 0:P], zeros16[0:EP, 0:n],
                               start=True, stop=False)
            mm.then_inc(s_sort_mm, SORT0)
            with pe.Fori(0, EC // SU) as i:
                for k in range(SU):
                    b, m = divmod(k, SB)
                    n = b * SM + m
                    if m < SM:
                        pe.wait_ge(s_hot, i * SR + (n + 1))
                        pe.wait_ge(s_ab, i * SR + (n + 1))
                        for ps, slot in ((sa_ps, slot_a), (sb_ps, slot_b)):
                            for half in range(2):
                                pe.matmul(ps[half][:, 0:HB], slot[:, n, :],
                                          tile_hot[:, n, half * HB:(half + 1) * HB],
                                          start=False, stop=False)
                    pe.matmul(cnt_ps[:, 0:R * NW], node_hot[:, b, m, :], rw_hot[:, b, m, :],
                              start=False, stop=False).then_inc(s_sort_mm, 1)
            for ps, n in sums:
                mm = pe.matmul(ps[:, 0:n], zeros16[0:EP, 0:P], zeros16[0:EP, 0:n],
                               start=False, stop=True)
            mm.then_inc(s_sorted, 1)
            pe.wait_ge(s_inv, 1)
            pe.transpose(inv_ps[0:R * NW, 0:P], inv[:, :], ident[:, :]).then_inc(s_inv_t, 1)
            pe.wait_ge(s_decoded, 1)

            for q in range(L + 1):
                aggregate(q)

        @block.scalar
        def _(act):
            act.sem_inc(s_xt, BUF)
            act.sem_inc(s_xc, ONE0)
            act.sem_inc(s_xe, ONE0)
            act.sem_inc(s_ev, ONE0)
            act.sem_inc(s_hs, 16)
            act.sem_inc(s_x1w, 16)
            act.sem_inc(s_hev, BUF)

            def copy_transpose(c, j):
                act.wait_ge(s_tp, c * CW + (j + 1))
                act.wait_ge(s_hmm, c * CW + (BUF + j - 1))
                act.copy(xt[:, SLOT[j % CW], :], xt_ps[j % CW % 2][:, 0:D]).then_inc(s_xt, 1)

            def copy_chunk(c, last=False):
                for j in range(CW):
                    if not (last and j == CW - 1):
                        copy_transpose(c, j + 1)
                    act.wait_ge(s_hmm, c * CW + (BUF + j + 1))
                    act.copy(cols(acc, c * CD + j * D, D), w0_ps[SLOT[j]][:, 0:D]
                             ).then_inc(s_hev, 1)

            def copy_row_numbers(q, g, c, table):
                act.wait_ge(s_mm, g * BODY + (q * NT + MM0 + (c - 3) * QT))
                act.copy(idx[:, c % 4 * QT:(c % 4 + 1) * QT],
                         cols(table, g * BODY + c * QT, QT)).then_inc(s_idx, 1)

            def edge_matrices(t, k0, before, between=None):
                if between or before:
                    act.wait_ge(s_em, before * HALF)
                for i in range(HALF):
                    a = act.activation(square[:, i * P:(i + 1) * P], iota[:, 0:P], ACT.Square,
                                       bias=cols(neg_node, t + i, 1))
                a.then_inc(s_sq, 1)
                act.wait_ge(s_sq, before + 1)
                for i in range(HALF):
                    if between:
                        act.wait_ge(s_mm, t + (MM0 + i + 1 - BODY))
                        if i in between:
                            between[i]()
                    act.activation(emat[:, k0 + i, :], square[:, i * P:(i + 1) * P], ACT.Relu,
                                   bias=ones[:, 0:1], scale=-1.0).then_inc(s_em, 1)

            def window_sd(n):
                act.wait_ge(s_var, n + 1)
                act.activation(wsd[:, :], wmv[:, 1:2], ACT.Sqrt, bias=eps_col[:, :]
                               ).then_inc(s_wsd, 1)

            def first_norm(n):
                act.wait_ge(s_nmr, n + 1)
                act.wait_ge(s_x1w, (n + ONE0) * 16)
                act.activation(x_win, y_win, ACT.Identity, bias=wnmr[:, :], scale=wrstd[:, :]
                               ).then_inc(s_xn, 1)

            def window_exp(m):
                act.wait_ge(s_min, m + 1)
                act.activation(e_win, e_win, ACT.Exp).then_inc(s_exp, 1)

            def window_features(n, v):
                act.wait_ge(s_xn, n + 1)
                act.copy(cols(X, v * D, D), x_win).then_inc(s_xc, 1)

            def window_transposed(n):
                act.wait_ge(s_tw, n + 1)
                act.copy(xt[:, 0, :], win_t_ps[:, 0:D]).then_inc(s_xe, 1)

            def window_products_out(n, v):
                act.wait_ge(s_hm, n + 1)
                act.wait_ge(s_hs, (n + 1) * 16)
                for h in range(2):
                    act.copy(hout[:, 0, 2 * h * D:2 * (h + 1) * D], win_ps[h][:, :])
                act.copy(cols(acc, v * D, D), root_ps[:, 0:D]).then_inc(s_ev, 1)

            def final_sd(j):
                act.wait_ge(s_fin, j * NFIN + 4)
                act.activation(wsd[:, :], wmv[:, 1:2], ACT.Sqrt, bias=eps_col[:, :]
                               ).then_inc(s_fsd, 1)

            def serve_messages(q, last=False):
                for c in range(3):
                    copy_row_numbers(q, 0, c, g_rel)
                for c in range(3, 7):
                    copy_row_numbers(q, 0, c, g_rel)
                with act.Fori(1, NB) as g:
                    n = g + (q * NW - 1)
                    v = window_at(mybir.EngineType.Activation, g - 1)
                    copy_row_numbers(q, g, 3, g_rel)
                    window_sd(n)
                    copy_row_numbers(q, g, 4, g_rel)
                    window_exp(g + ((q - 1) * NW - 1))
                    copy_row_numbers(q, g, 5, g_rel)
                    if last:
                        final_sd(g - 1)
                    else:
                        window_features(n, v)
                        window_transposed(n)
                    copy_row_numbers(q, g, 6, g_rel)
                    if not last:
                        window_products_out(n, v)
                n = (q + 1) * NW - 1
                window_sd(n)
                window_exp(q * NW - 1)
                if last:
                    final_sd(NW - 1)
                else:
                    v = window_at(mybir.EngineType.Activation, NW - 1)
                    window_features(n, v)
                    window_transposed(n)
                    window_products_out(n, v)

            def serve_first(g, work, v=None):
                n = g - 1
                copy_row_numbers(0, g, 3, g_src)

                def middle():
                    copy_row_numbers(0, g, 4, g_src)
                    if work:
                        window_sd(n)

                def features():
                    if work:
                        first_norm(n)
                        window_features(n, v)

                edge_matrices(g * BODY + BODY, 0, g * 2 + 2, {QT: middle, 13: features})
                copy_row_numbers(0, g, 5, g_src)
                if work:
                    window_transposed(n)
                edge_matrices(g * BODY + (BODY + HALF), HALF, g * 2 + 3,
                              {QT: lambda: copy_row_numbers(0, g, 6, g_src)})
                if work:
                    window_products_out(n, v)

            copy_transpose(0, 0)
            with act.Fori(0, NC - 1) as c:
                copy_chunk(c)
            copy_chunk(NC - 1, last=True)
            act.wait_ge(s_lane, 1)
            def edge_values(i, again):
                for b in range(2):
                    if again:
                        act.wait_ge(s_scat[b], i * (16 * SS))
                    act.copy(idx[0:EP, b * SS:(b + 1) * SS],
                             row[:, bass.ds(i * SU + (b * SB + SM), SS)])
                    act.copy(leaving[:, b * SS:(b + 1) * SS, :],
                             record[:, bass.ds(i * SU + (b * SB + SM), SS), :]
                             ).then_inc(s_rows, 1)
                    act.wait_ge(s_lane, i * 2 + (b + 2))
                    for m in range(SM):
                        k, n = b * SB + m, b * SM + m
                        act.wait_ge(s_sort_mm, i * SU + (SORT0 + k + 1 - SU))
                        for slot, val in ((slot_a, val_a), (slot_b, val_b)):
                            a = act.activation(slot[:, n, :], lane_hot[:, b, m, :], ACT.Copy,
                                               scale=val[:, bass.ds(i * SU + k, 1)])
                        a.then_inc(s_ab, 1)
            edge_values(0, False)
            with act.Fori(1, EC // SU) as i:
                edge_values(i, True)
            act.wait_ge(s_deg, 1)
            act.activation(deg_s[:, :], deg1[:, :], ACT.Sqrt).then_inc(s_degs, 1)
            act.wait_ge(s_dis, 1)

            def scale_rows(c, reused):
                for j in range(CW):
                    if reused:
                        act.wait_ge(s_hw[j], c * 16)
                    act.activation(hout[:, j, 0:D], cols(acc, c * CD + j * D, D), ACT.Copy,
                                   scale=cols(dis, c * CW + j, 1)).then_inc(s_h0, 1)

            scale_rows(0, False)
            with act.Fori(1, NC) as c:
                scale_rows(c, True)
            act.wait_ge(s_decoded, 1)
            for c in range(3):
                copy_row_numbers(0, 0, c, g_src)
            for j in range(CW):
                act.wait_ge(s_hw[j], 16 * NC)
            edge_matrices(0, 0, 0)
            edge_matrices(HALF, HALF, 1)
            serve_first(0, False)
            with act.Fori(1, NB) as g:
                serve_first(g, True, window_at(mybir.EngineType.Activation, g - 1))
            v = window_at(mybir.EngineType.Activation, NW - 1)
            window_sd(NW - 1)
            first_norm(NW - 1)
            window_features(NW - 1, v)
            window_transposed(NW - 1)
            window_products_out(NW - 1, v)
            for q in range(1, L):
                serve_messages(q)
            serve_messages(L, last=True)

        @block.vector
        def _(dve):
            steps = [0]

            def done(ins, more=0):
                steps[0] += 1
                ins.then_inc(s_dve, 1)
                dve.wait_ge(s_dve, more + steps[0])

            dve.wait_ge(s_edges, 48)
            dve.wait_ge(s_const, 1)
            done(dve.tensor_scalar(t1_i, dst_i, 7, None, ALU.arith_shift_right))
            dve.tensor_copy(d_hi, t1_i)
            done(dve.scalar_tensor_tensor(rel_win[:, 0:EC], typ_i, float(NW), t1_i,
                                          ALU.mult, ALU.add))
            done(dve.tensor_scalar(t1_i, dst_i, P - 1, None, ALU.bitwise_and))
            dve.tensor_copy(d_lo[:, 0:EC], t1_i)
            done(dve.tensor_scalar(t1_i, t1_i, 3, None, ALU.logical_shift_left))
            done(dve.tensor_scalar(t2_i, src_i, LOWBITS, None, ALU.arith_shift_right))
            done(dve.tensor_tensor(t1_i, t1_i, t2_i, ALU.bitwise_or))
            done(dve.tensor_scalar(val_b, t1_i, 1.0, None, ALU.add))
            done(dve.tensor_scalar(t2_i, src_i, LOW - 1, 2, ALU.bitwise_and,
                                   ALU.logical_shift_left))
            done(dve.tensor_tensor(t2_i, t2_i, typ_i, ALU.bitwise_or))
            dve.memset(d_lo[:, EC:EX], 0.0)
            dve.memset(rel_win[:, EC:EX], 0.0)
            dve.memset(pos_lo[:, EC:EX], 0.0)
            done(dve.tensor_copy(val_a, t2_i))
            done(dve.memset(one_row, 1.0))
            with dve.Fori(0, NW // CW) as i:
                for j in range(CW):
                    w = i * CW + j
                    dve.tensor_scalar(hits[SLOT[j]], d_hi, iota[0:EP, bass.ds(w, 1)], None,
                                      ALU.is_equal, ALU.add, accum_out=tot[0:EP, bass.ds(w, 1)]
                                      ).then_inc(s_dve, 1)
                    dve.wait_ge(s_dve, w + (steps[0]))
            steps[0] += NW
            dve.wait_ge(s_dve, steps[0])
            done(dve.memset(pos, 0.0))
            dve.sem_inc(s_tot, 1)
            dve.wait_ge(s_base, 1)
            done(dve.tensor_scalar(n_tiles_i[:, :], misc_ps[:, 64:64 + NW], float(P - 1), None,
                                   ALU.add))
            done(dve.tensor_scalar(n_tiles_i[:, :], n_tiles_i[:, :], 7, None,
                                   ALU.arith_shift_right))
            done(dve.tensor_copy(n_tiles[:, :], n_tiles_i[:, :]))
            by_window = (lambda a: a[:, :].rearrange("p (w v) -> p w v", v=1)
                         .to_broadcast([P, NW, NW]))
            over_windows = (lambda a: a.rearrange("p (w v) -> p w v", w=1)
                            .to_broadcast([P, NW, NW]))
            done(dve.scalar_tensor_tensor(size_key[:, :], n_tiles[:, :], 32.0, iota[:, 0:NW],
                                          ALU.mult, ALU.add))
            done(dve.tensor_tensor(pair_a, over_windows(size_key[:, :]), by_window(size_key),
                                   ALU.is_lt))
            done(dve.tensor_reduce(place[:, :], pair_a, AXX, ALU.add))
            done(dve.tensor_tensor(pair_a, pair_a, over_windows(n_tiles[:, :]), ALU.mult))
            done(dve.tensor_reduce(t_start[:, :], pair_a, AXX, ALU.add))
            done(dve.tensor_tensor(pair_a, over_windows(place[:, :]), by_window(iota[:, 0:NW]),
                                   ALU.is_equal))
            done(dve.tensor_tensor(pair_b, pair_a, over_windows(iota[:, 0:NW]), ALU.mult))
            done(dve.tensor_reduce(order[:, :], pair_b, AXX, ALU.add))
            done(dve.tensor_tensor(pair_b, pair_a, over_windows(t_start[:, :]), ALU.mult))
            done(dve.tensor_reduce(t_first[:, :], pair_b, AXX, ALU.add))
            done(dve.tensor_copy(order_i[:, :], order[0:1, :]))
            done(dve.tensor_copy(order_step[:, 0:1], order[:, 0:1]))
            done(dve.tensor_tensor(order_step[:, 1:NW], order[:, 1:NW], order[:, 0:NW - 1],
                                   ALU.subtract))
            done(dve.scalar_tensor_tensor(run0[0:EP, :], t_start[0:EP, :], float(P),
                                          misc_ps[0:EP, 0:NW], ALU.mult, ALU.add))
            done(dve.tensor_scalar(run0[0:EP, :], run0[0:EP, :], -1.0, None, ALU.add))
            dve.sem_inc(s_pos0, 1)
            done(dve.tensor_tensor(pick[:, :], ident[0:NW, 0:NW], order_step[0:NW, :], ALU.mult))
            done(dve.tensor_reduce(order_col[:, :], pick[:, :], AXX, ALU.add))
            done(dve.tensor_tensor(pick[:, :], ident[0:NW, 0:NW], t_first[0:NW, :], ALU.mult))
            done(dve.tensor_reduce(first_col[:, :], pick[:, :], AXX, ALU.add))
            dve.tensor_scalar(win_ge, iota16[0:NW, :], first_col[:, :], None, ALU.is_ge
                              ).then_inc(s_wcol, 1)

            def hit_row(w, slot):
                return dve.tensor_scalar(hits[slot], d_hi, iota[0:EP, bass.ds(w, 1)], None,
                                         ALU.is_equal)

            dve.sem_inc(s_rank, 1)
            done(hit_row(0, 0))
            with dve.Fori(0, NW // CW) as i:
                before_body = i * (2 * CW) + steps[0]
                for j in range(CW):
                    w = i * CW + j
                    run, hit = runs[SLOT[j]], hits[SLOT[j]]
                    dve.wait_ge(s_ranked, w + (BUF - 1))
                    dve.wait_ge(s_dve, before_body + 2 * j)
                    dve.tensor_tensor_scan(run, one_row, hit, run0[0:EP, bass.ds(w, 1)],
                                           ALU.mult, ALU.add).then_inc(s_dve, 1)
                    dve.wait_ge(s_rank, w + 1)
                    hit_row(w + 1, SLOT[(j + 1) % CW]).then_inc(s_dve, 1)
                    dve.wait_ge(s_dve, before_body + (2 * j + 1))
                    dve.tensor_tensor(run, run, hit, ALU.mult).then_inc(s_rank, 1)
            steps[0] += 2 * NW
            dve.wait_ge(s_ranked, BUF + NW)
            done(dve.tensor_copy(t1_i, pos))
            done(dve.tensor_scalar(t2_i, t1_i, 7, None, ALU.arith_shift_right))
            done(dve.tensor_copy(pos_hi, t2_i))
            done(dve.tensor_scalar(t2_i, t1_i, P - 1, None, ALU.bitwise_and))
            done(dve.tensor_copy(pos_lo[:, 0:EC], t2_i))
            dve.scalar_tensor_tensor(row, pos_lo[:, 0:EC], float(NT), pos_hi, ALU.mult, ALU.add
                                     ).then_inc(s_lane, 1)
            dve.wait_ge(s_wmm, 1)
            for half in range(2):
                c = dve.tensor_copy(win_i[:, half * HB:(half + 1) * HB],
                                    banks[6 + half][0:1, 0:HB])
            c.then_inc(s_win, 1)
            dve.wait_ge(s_cleared, 16)

            def spread(v, t, n, s=SB):
                return (v[:, bass.ds(t, s)].rearrange("p (s n) -> p s n", n=1)
                        .to_broadcast([EP, s, n]))

            def lanes(n, s=SB):
                return (iota16[0:EP, 0:n].rearrange("p (s n) -> p s n", s=1)
                        .to_broadcast([EP, s, n]))

            def lane_part(b, t):
                dve.tensor_tensor(lane_hot[:, b, 0:SM, :], lanes(P, SM),
                                  spread(pos_lo, t, P, SM), ALU.is_equal).then_inc(s_lane, 1)

            def node_part(b, t):
                dve.tensor_tensor(node_hot[:, b, :, :], lanes(P), spread(d_lo, t, P),
                                  ALU.is_equal)

            def window_part(b, t):
                dve.tensor_tensor(rw_hot[:, b, :, :], lanes(R * NW),
                                  spread(rel_win, t, R * NW), ALU.is_equal)

            parts = (lane_part, node_part, window_part)
            for part in parts:
                part(0, 0)
            with dve.Fori(0, EC // SU) as i:
                for b in range(2):
                    t = i * SU + b * SB
                    for m in range(SM):
                        k, n = b * SB + m, b * SM + m
                        dve.wait_ge(s_sort_mm, i * SU + (SORT0 + k + 1 - SU))
                        dve.tensor_scalar(tile_hot[:, n, :], iota16[0:EP, :],
                                          pos_hi[:, bass.ds(t + m, 1)], None,
                                          ALU.is_equal).then_inc(s_hot, 1)
                        if m == 1:
                            dve.wait_ge(s_sort_mm, i * SU + (SORT0 + b * SB))
                        if m > 0:
                            parts[m - 1](1 - b, t + SB)
            dve.wait_ge(s_sorted, 1)
            dve.wait_ge(s_win, 1)
            done(dve.tensor_copy(cnt[:, :], cnt_ps[:, 0:R * NW]))
            done(dve.tensor_scalar(inv[:, :], cnt[:, :], 1.0, None, ALU.max))
            dve.reciprocal(inv[:, :], inv[:, :]).then_inc(s_inv, 1)
            done(dve.tensor_reduce(deg[:, :], cnt[:, :].rearrange("p (r w) -> p w r", r=R),
                                   AXX, ALU.add))
            dve.tensor_scalar(deg1[:, :], deg[:, :], 1.0, None, ALU.max).then_inc(s_deg, 1)
            dve.wait_ge(s_degs, 1)
            done(dve.reciprocal(deg_s[:, :], deg_s[:, :]))
            dve.scalar_tensor_tensor(dis[:, :], deg[:, :], 0.0, deg_s[:, :],
                                     ALU.is_gt, ALU.mult).then_inc(s_dis, 1)
            dve.wait_ge(s_inv_t, 1)
            dve.tensor_copy(inv_t[:, :], inv_ps[0:R * NW, 0:P]).then_inc(s_inv_s, 1)
            dve.wait_ge(s_back, 16)
            for b in range(2):
                half = slice(b * HB, (b + 1) * HB)
                dve.tensor_tensor(a_i[:, half], sa_ps[b][:, 0:HB], placed[:, half, 0], ALU.add)
                done(dve.scalar_tensor_tensor(b_i[:, half], sb_ps[b][:, 0:HB], -1.0,
                                              placed[:, half, 1], ALU.add, ALU.add))
            done(dve.tensor_scalar(c_i, b_i, 0, None, ALU.max))
            done(dve.tensor_scalar(b_i, b_i, 3, None, ALU.arith_shift_right))
            done(dve.memset(node[:, NT:MT], -1.0))
            done(dve.memset(weight[:, NT:MT], 0.0))
            done(dve.memset(g_src[:, NT:NI], 0))
            done(dve.memset(g_rel[:, NT:NI], 0))
            done(dve.tensor_copy(node[:, 0:NT], b_i))
            done(dve.tensor_scalar(neg_node[:, :], node[:, :], -1.0, None, ALU.mult))
            done(dve.tensor_scalar(c_i, c_i, 7, LOWBITS, ALU.bitwise_and,
                                   ALU.logical_shift_left))
            done(dve.tensor_scalar(b_i, a_i, 2, None, ALU.arith_shift_right))
            done(dve.tensor_tensor(g_src[:, 0:NT], b_i, c_i, ALU.bitwise_or))
            done(dve.tensor_scalar(a_i, a_i, 3, None, ALU.bitwise_and))
            dve.scalar_tensor_tensor(g_rel[:, 0:NT], a_i, float(NPAD), g_src[:, 0:NT],
                                     ALU.mult, ALU.add)
            dve.scalar_tensor_tensor(key[:, :], a_i, float(P), node[:, 0:NT],
                                     ALU.mult, ALU.add).then_inc(s_decoded, 1)
            dve.wait_ge(s_decoded, 1)
            dve.wait_ge(s_h0, NW)
            dve.memset(acc, 0.0).then_inc(s_acc, ACC0)

            def edge_matrix(t, k, free):
                if free is not None:
                    dve.wait_ge(s_mm, free)
                dve.tensor_scalar(emat[:, k % BODY, :], iota[:, 0:P], cols(node, t, 1),
                                  cols(weight, t, 1), ALU.is_equal, ALU.mult
                                  ).then_inc(s_em, 1)

            inv_v = inv_b.rearrange("p (r w d) -> p r w d", r=R, w=NW)
            key_v = iota[:, :].rearrange("p (r d) -> p r d", r=R)

            def add_tiles(q, g, tiles, work):
                for k0 in range(0, tiles, QT):
                    part = min(QT, tiles - k0)
                    _, wins = nc.values_load_multi_w_load_instructions(
                        win_i[0:1, bass.ds(g * BODY + k0, part)],
                        engines=[mybir.EngineType.DVE], min_val=0, max_val=NW - 1,
                        skip_runtime_bounds_check_because="a tile's window is below NW")
                    for i in range(part):
                        k = k0 + i
                        t = g * BODY + k
                        if q == 0:
                            dve.scalar_tensor_tensor(
                                found[:, k % 2, :, :], key_v, cols(key, t, 1),
                                inv_v[:, :, bass.ds(wins[i], 1), :]
                                .rearrange("p r w d -> p r (w d)"),
                                ALU.is_equal, ALU.mult, accum_out=cols(weight, t, 1))
                        elif tiles == BODY:
                            edge_matrix(t + HALF, k + HALF,
                                        g * BODY + (q * NT + MM0 + k + HALF + 1 - BODY))
                        dve.wait_ge(s_mm, g * BODY + (q * NT + MM0 + k + 1))
                        dve.wait_ge(s_acc, g * BODY + (q * NT + ACC0 + k))
                        a = cols(acc, wins[i] * D, D)
                        dve.tensor_tensor(a, a, agg_ps[k % NPS][:, 0:D], ALU.add
                                          ).then_inc(s_acc, 1)
                        if k in work:
                            work[k]()

            def first_work(g, v):
                n = g - 1

                def after(i):
                    dve.wait_ge(s_first, n * NFIRST + i)

                def scaled():
                    dve.wait_ge(s_acc, g * BODY + (ACC0 + REST))
                    dve.wait_ge(s_xc, n + ONE0)
                    dve.scalar_tensor_tensor(y_win, cols(acc, v * D, D), cols(dis, v, 1),
                                             cols(X, v * D, D), ALU.mult, ALU.add
                                             ).then_inc(s_first, 1)

                def partial():
                    after(1)
                    dve.bn_stats(wstats[:, :], y_win).then_inc(s_first, 1)

                def variance():
                    after(2)
                    apart(dve)
                    dve.bn_aggr(wmv[:, :], wstats[:, :]).then_inc(s_var, 1)

                def inverse():
                    dve.wait_ge(s_wsd, n + 1)
                    dve.reciprocal(wrstd[:, :], wsd[:, :]).then_inc(s_first, 1)
                    after(3)
                    dve.wait_ge(s_var, n + 1)
                    dve.scalar_tensor_tensor(wnmr[:, :], wmv[:, 0:1], -1.0, wrstd[:, :],
                                             ALU.mult, ALU.mult).then_inc(s_nmr, 1)

                return {5: scaled, 6: partial, 7: variance, 11: inverse}

            def window_work(q, g, v):
                m = g + ((q - 1) * NW - 1)
                n = g + (q * NW - 1)
                a, x_old = cols(acc, v * D, D), cols(X, v * D, D)
                mean_, var_in = wmv[:, 0:1], wstats[:, :]

                def step(ins):
                    ins.then_inc(s_step, 1)

                def after(i):
                    dve.wait_ge(s_step, m * NSTEP + i)

                def partial():
                    dve.wait_ge(s_acc, g * BODY + (q * NT + ACC0 + REST))
                    step(dve.bn_stats(var_in, a))

                def variance():
                    after(1)
                    apart(dve)
                    dve.bn_aggr(wmv[:, :], var_in).then_inc(s_var, 1)

                def inverse():
                    dve.wait_ge(s_wsd, n + 1)
                    step(dve.reciprocal(wrstd[:, :], wsd[:, :]))

                def centre():
                    dve.wait_ge(s_gb, q * 32)
                    dve.wait_ge(s_var, n + 1)
                    step(dve.scalar_tensor_tensor(y_win, a, mean_, gamma_sb[:, :],
                                                  ALU.subtract, ALU.mult))

                def scale():
                    after(3)
                    step(dve.scalar_tensor_tensor(y_win, y_win, wrstd[:, :], beta_sb[:, :],
                                                  ALU.mult, ALU.add))

                def negative():
                    after(4)
                    dve.tensor_scalar(e_win, y_win, 0.0, None, ALU.min).then_inc(s_min, 1)

                def elu():
                    dve.wait_ge(s_exp, m + 1)
                    step(dve.scalar_tensor_tensor(y_win, y_win, 0.0, e_win, ALU.max, ALU.add))

                def residual():
                    after(5)
                    dve.wait_ge(s_xc, n + ONE0)
                    dve.wait_ge(s_xe, n + ONE0)
                    dve.scalar_tensor_tensor(x_win, y_win, -1.0, x_old, ALU.add, ALU.add
                                             ).then_inc(s_xn, 1)

                work = {5: partial, 6: variance, 9: inverse, 10: centre, 11: scale,
                        12: negative, 15: elu, 16: residual}
                if q < L:
                    return work

                def own(i):
                    dve.wait_ge(s_fin, (g - 1) * NFIN + i)

                def sum_of_layers():
                    after(5)
                    dve.scalar_tensor_tensor(e_win, y_win, -1.0, x_old, ALU.add, ALU.add
                                             ).then_inc(s_fin, 1)
                    own(1)
                    dve.wait_ge(s_x1, 16)
                    dve.tensor_tensor(x_win, e_win, cols(X1, v * D, D), ALU.add
                                      ).then_inc(s_fin, 1)

                def final_variance():
                    own(2)
                    dve.bn_stats(var_in, x_win).then_inc(s_fin, 1)
                    own(3)
                    apart(dve)
                    dve.bn_aggr(wmv[:, :], var_in).then_inc(s_fin, 1)

                def final_inverse():
                    dve.wait_ge(s_fsd, g)
                    dve.reciprocal(wrstd[:, :], wsd[:, :]).then_inc(s_fin, 1)

                def final_norm():
                    own(5)
                    dve.tensor_scalar(a, x_win, mean_, wrstd[:, :], ALU.subtract, ALU.mult
                                      ).then_inc(s_outn, 1)

                work.update({16: sum_of_layers, 18: final_variance, 21: final_inverse,
                             22: final_norm})
                return work

            def messages(q):
                if q == 0:
                    dve.wait_ge(s_inv_b, 16)
                else:
                    for k in range(HALF):
                        edge_matrix(k, k, None)
                    dve.wait_ge(s_ev, q * NW + ONE0)
                work = (lambda g, v: window_work(q, g, v)) if q else first_work
                add_tiles(q, 0, BODY, {})
                with dve.Fori(1, NB) as g:
                    add_tiles(q, g, BODY, work(g, window_at(mybir.EngineType.DVE, g - 1)))
                add_tiles(q, NB, REST, {})
                for part in work(NB, window_at(mybir.EngineType.DVE, NW - 1)).values():
                    part()

            for q in range(L + 1):
                messages(q)


_INS = ['x', 'src', 'dst', 'edge_type_4', 'L0_gnn_W', 'L1_gnn_weights', 'L1_gnn_roots',
        'L1_gnn_biases', 'L1_gnn_ln_gamma', 'L1_gnn_ln_beta']


def kernel(**inputs):
    import numpy as _np
    import concourse.bacc as _bacc
    from concourse.bass_utils import run_bass_kernel_spmd as _run

    f32 = mybir.dt.float32
    nc = _bacc.Bacc("TRN2", target_bir_lowering=False, num_devices=1)
    arrays, args = {}, []
    for name in _INS:
        a = _np.ascontiguousarray(inputs[name])
        arrays[f"in_{name}_dram"] = a
        args.append(nc.dram_tensor(f"in_{name}_dram", a.shape, mybir.dt.from_np(a.dtype),
                                   kind="ExternalInput").ap())
    n, d = inputs['x'].shape
    r = inputs['L1_gnn_weights'].shape[1]
    rows = -(-n // 128) * 128
    out = nc.dram_tensor("out_0_dram", (n, d), f32, kind="ExternalOutput").ap()
    h0_table = nc.dram_tensor("h0_table", (rows, d), f32, kind="Internal").ap()
    h_tables = [nc.dram_tensor(f"h_table{i}", (r * rows, d), f32, kind="Internal").ap()
                for i in range(2)]
    inv_dram = nc.dram_tensor("inv_dram", (r * rows // 128, 128), f32, kind="Internal").ap()
    x1_dram = nc.dram_tensor("x1_dram", (rows, d), f32, kind="Internal").ap()
    tiles = (inputs['src'].shape[0] + (rows // 128) * 127) // 128
    placed = nc.dram_tensor("placed_dram", (128 * tiles, 2), f32, kind="Internal").ap()
    build_program(nc, *args, out, h0_table, h_tables, inv_dram, x1_dram, placed)
    res = _run(nc, [arrays], core_ids=[0])
    return res.results[0]["out_0_dram"]
```
